# Optimizing a Trainium2 kernel written in Bass

```python
import numpy as np
import jax
import jax.numpy as jnp

def _softmax(x, axis=-1):
    return jax.nn.softmax(x, axis=axis)

def _gelu(x):
    return jax.nn.gelu(x, approximate=True)

def _silu(x):
    return jax.nn.silu(x)

def _sigmoid(x):
    return jax.nn.sigmoid(x)

def _layernorm(x, axis=-1, eps=1e-05):
    m = jnp.mean(x, axis=axis, keepdims=True)
    v = jnp.var(x, axis=axis, keepdims=True)
    return (x - m) / jnp.sqrt(v + eps)

def _scatter_add(tgt, idx, src, axis=0):
    return tgt.at[idx].add(src)

def _segment_sum(src, seg, n):
    return jax.ops.segment_sum(src, seg, n)
kernel_name = 'mk_adaln_attn_ffn_d1_seqx_r4_2db937'

def setup_inputs(seed: int=0):
    np.random.seed(seed)
    _w = jnp.asarray

    def _rec_inputs():
        import jax
        import jax.numpy as jnp
        _rk = jax.random.key(seed)
        x = -0.000125 + 0.9999 * jax.random.normal(jax.random.fold_in(_rk, 1), (32, 64, 1024), jnp.float32)
        _lenS = 64 - jax.random.randint(jax.random.fold_in(_rk, 7), (32,), 0, max(1, 64 // 4) + 1, jnp.int32)
        _lenS2 = 64 - jax.random.randint(jax.random.fold_in(_rk, 8), (32,), 0, max(1, 64 // 4) + 1, jnp.int32)
        cond_128 = 0.0061147 + 1.02565 * jax.random.normal(jax.random.fold_in(_rk, 11), (32, 128), jnp.float32)
        fside_S_0 = -0.022604 + 0.987366 * jax.random.normal(jax.random.fold_in(_rk, 12), (64,), jnp.float32)
        return (x, cond_128, fside_S_0)
    x, cond_128, fside_S_0 = _rec_inputs()

    def _L0_cond_setup():
        import jax, jax.numpy as jnp
        import numpy as np
        K = 8
        T = 1.0
        D_EMBD = 128
        IN_C = 64
        OUT_C = 64
        BS = 32
        H = 1024
        HID = 128
        key = jax.random.key(seed)
        ks = jax.random.split(key, 10)
        s = lambda fan_in: 1.0 / np.sqrt(fan_in)
        return {'x': jax.random.normal(ks[0], (BS, IN_C, H), dtype=jnp.float32), 'embedding': jax.random.normal(ks[1], (BS, D_EMBD), dtype=jnp.float32), 'W0': jax.random.normal(ks[2], (D_EMBD, HID), dtype=jnp.float32) * s(D_EMBD), 'b0': jnp.zeros((HID,), dtype=jnp.float32), 'W1': jax.random.normal(ks[3], (HID, HID), dtype=jnp.float32) * s(HID), 'b1': jnp.zeros((HID,), dtype=jnp.float32), 'W2': jax.random.normal(ks[4], (HID, K), dtype=jnp.float32) * s(HID), 'b2': jnp.zeros((K,), dtype=jnp.float32), 'weight': jax.random.normal(ks[5], (K, OUT_C, IN_C, 1), dtype=jnp.float32) * s(IN_C), 'bias_k': jax.random.normal(ks[6], (K, OUT_C), dtype=jnp.float32) * 0.1}
    _L0_cond_all = _L0_cond_setup()
    _L0_cond_in = {k: v for k, v in _L0_cond_all.items() if k in ('W0', 'b0', 'W1', 'b1', 'W2', 'b2', 'weight', 'bias_k')}
    del _L0_cond_all

    def _L0_attn_setup():
        import jax, jax.numpy as jnp
        import numpy as np
        N_HEAD = 32
        ROPE_BASE = 10000.0

        def _rope_cos_sin(T, n_elem, dtype):
            theta = 1.0 / ROPE_BASE ** (jnp.arange(0, n_elem, 2, dtype=dtype) / n_elem)
            seq_idx = jnp.arange(T, dtype=dtype)
            idx_theta = jnp.outer(seq_idx, theta)
            idx_theta2 = jnp.concatenate([idx_theta, idx_theta], axis=-1)
            return (jnp.cos(idx_theta2), jnp.sin(idx_theta2))

        def _apply_rope(x, cos, sin):
            d2 = x.shape[-1] // 2
            rot = jnp.concatenate([-x[..., d2:], x[..., :d2]], axis=-1)
            return x * cos + rot * sin
        key = jax.random.key(seed)
        k1, k2, k3, k4 = jax.random.split(key, 4)
        B, T, C = (1, 512, 1024)
        s_in = 1.0 / np.sqrt(C)
        return {'x': jax.random.normal(k1, (B, T, C), jnp.float32), 'w_attn': jax.random.normal(k2, (3 * C, C), jnp.float32) * s_in, 'w_proj': jax.random.normal(k3, (C, C), jnp.float32) * s_in, 'adapter_wte': jax.random.normal(k4, (10, C), jnp.float32), 'gating': jnp.ones((1,), jnp.float32)}
    _L0_attn_all = _L0_attn_setup()
    _L0_attn_in = {k: v for k, v in _L0_attn_all.items() if k in ('w_attn', 'w_proj', 'adapter_wte', 'gating')}
    del _L0_attn_all

    def _L0_cond2_setup():
        import jax, jax.numpy as jnp
        import numpy as np
        from jax import lax
        N, C_IN, L = (32, 64, 1024)
        C_OUT, K, GROUPS = (64, 9, 4)
        C_DIM, PAD, STRIDE = (128, 4, 1)
        key = jax.random.key(seed)
        k1, k2, k3, k4, k5 = jax.random.split(key, 5)
        x = jax.random.normal(k1, (N, C_IN, L), dtype=jnp.float32)
        c = jax.random.normal(k2, (N, C_DIM), dtype=jnp.float32)
        weight = jax.random.normal(k3, (C_OUT, C_IN // GROUPS, K), dtype=jnp.float32)
        c_weight = jax.random.normal(k4, (C_OUT, C_DIM), dtype=jnp.float32)
        bias = jax.random.normal(k5, (C_OUT,), dtype=jnp.float32)
        return {'x': x, 'c': c, 'weight': weight, 'c_weight': c_weight, 'bias': bias}
    _L0_cond2_all = _L0_cond2_setup()
    _L0_cond2_in = {k: v for k, v in _L0_cond2_all.items() if k in ('weight', 'c_weight')}
    del _L0_cond2_all

    def _L0_ffn_setup():
        import jax, jax.numpy as jnp
        import numpy as np
        NUM_EXPERTS = 8
        TOP_K = 2
        RANK = 16
        LORA_ALPHA = 32
        SCALING = LORA_ALPHA / RANK
        key = jax.random.key(seed)
        ks = jax.random.split(key, 6)
        B, S, D_IN, D_OUT = (4, 512, 1024, 1024)
        x = jax.random.normal(ks[0], (B, S, D_IN), dtype=jnp.float32)
        W_base = jax.random.normal(ks[1], (D_OUT, D_IN), dtype=jnp.float32) * 0.02
        b_base = jax.random.normal(ks[2], (D_OUT,), dtype=jnp.float32) * 0.02
        W_router = jax.random.normal(ks[3], (NUM_EXPERTS, D_IN), dtype=jnp.float32) * 0.02
        A = jax.random.normal(ks[4], (NUM_EXPERTS, RANK, D_IN), dtype=jnp.float32) * 0.02
        Bm = jax.random.normal(ks[5], (D_OUT, RANK), dtype=jnp.float32) * 0.02
        Bm = jnp.broadcast_to(Bm, (NUM_EXPERTS, D_OUT, RANK)) * jnp.arange(1, NUM_EXPERTS + 1, dtype=jnp.float32)[:, None, None] * 0.2
        return {'x': x, 'W_base': W_base, 'b_base': b_base, 'W_router': W_router, 'A': A, 'B': Bm}
    _L0_ffn_all = _L0_ffn_setup()
    _L0_ffn_in = {k: v for k, v in _L0_ffn_all.items() if k in ('W_base', 'b_base', 'W_router', 'A', 'B')}
    del _L0_ffn_all
    return {'x': x, 'cond_128': cond_128, 'fside_S_0': fside_S_0, 'L0_cond_W0': _L0_cond_in['W0'], 'L0_cond_b0': _L0_cond_in['b0'], 'L0_cond_W1': _L0_cond_in['W1'], 'L0_cond_b1': _L0_cond_in['b1'], 'L0_cond_W2': _L0_cond_in['W2'], 'L0_cond_b2': _L0_cond_in['b2'], 'L0_cond_weight': _L0_cond_in['weight'], 'L0_cond_bias_k': _L0_cond_in['bias_k'], 'L0_attn_w_attn': _L0_attn_in['w_attn'], 'L0_attn_w_proj': _L0_attn_in['w_proj'], 'L0_attn_adapter_wte': _L0_attn_in['adapter_wte'], 'L0_attn_gating': _L0_attn_in['gating'], 'L0_cond2_weight': _L0_cond2_in['weight'], 'L0_cond2_c_weight': _L0_cond2_in['c_weight'], 'L0_ffn_W_base': _L0_ffn_in['W_base'], 'L0_ffn_b_base': _L0_ffn_in['b_base'], 'L0_ffn_W_router': _L0_ffn_in['W_router'], 'L0_ffn_A': _L0_ffn_in['A'], 'L0_ffn_B': _L0_ffn_in['B']}

def reference(x, cond_128, fside_S_0, L0_cond_W0, L0_cond_b0, L0_cond_W1, L0_cond_b1, L0_cond_W2, L0_cond_b2, L0_cond_weight, L0_cond_bias_k, L0_attn_w_attn, L0_attn_w_proj, L0_attn_adapter_wte, L0_attn_gating, L0_cond2_weight, L0_cond2_c_weight, L0_ffn_W_base, L0_ffn_b_base, L0_ffn_W_router, L0_ffn_A, L0_ffn_B):
    import jax
    import jax.numpy as jnp

    def _L0_cond_ref(x, embedding, W0, b0, W1, b1, W2, b2, weight, bias_k):
        import jax, jax.numpy as jnp
        import numpy as np
        K = 8
        T = 1.0
        D_EMBD = 128
        IN_C = 64
        OUT_C = 64
        BS = 32
        H = 1024
        HID = 128
        h = jax.nn.gelu(embedding @ W0 + b0, approximate=False)
        h = jax.nn.gelu(h @ W1 + b1, approximate=False)
        att = jax.nn.softmax((h @ W2 + b2) / T, axis=-1)
        agg_w = jnp.einsum('bk,koi->boi', att, weight[..., 0])
        agg_b = att @ bias_k
        out = jnp.einsum('boi,bih->boh', agg_w, x) + agg_b[:, :, None]
        return out

    def _L0_attn_ref(x, w_attn, w_proj, adapter_wte, gating):
        import jax, jax.numpy as jnp
        import numpy as np
        N_HEAD = 32
        ROPE_BASE = 10000.0

        def _rope_cos_sin(T, n_elem, dtype):
            theta = 1.0 / ROPE_BASE ** (jnp.arange(0, n_elem, 2, dtype=dtype) / n_elem)
            seq_idx = jnp.arange(T, dtype=dtype)
            idx_theta = jnp.outer(seq_idx, theta)
            idx_theta2 = jnp.concatenate([idx_theta, idx_theta], axis=-1)
            return (jnp.cos(idx_theta2), jnp.sin(idx_theta2))

        def _apply_rope(x, cos, sin):
            d2 = x.shape[-1] // 2
            rot = jnp.concatenate([-x[..., d2:], x[..., :d2]], axis=-1)
            return x * cos + rot * sin
        B, T, C = x.shape
        H = N_HEAD
        hd = C // H
        qkv = jnp.einsum('btc,oc->bto', x, w_attn)
        q, k, v = jnp.split(qkv, 3, axis=-1)
        q = q.reshape(B, T, H, hd).transpose(0, 2, 1, 3)
        k = k.reshape(B, T, H, hd).transpose(0, 2, 1, 3)
        v = v.reshape(B, T, H, hd).transpose(0, 2, 1, 3)
        cos, sin = _rope_cos_sin(T, hd, x.dtype)
        q = _apply_rope(q, cos, sin)
        k = _apply_rope(k, cos, sin)
        scores = jnp.einsum('bhqd,bhkd->bhqk', q, k) / jnp.sqrt(jnp.asarray(hd, x.dtype))
        causal = jnp.tril(jnp.ones((T, T), bool))
        scores = jnp.where(causal, scores, jnp.asarray(-jnp.inf, x.dtype))
        attn = jax.nn.softmax(scores, axis=-1)
        y = jnp.einsum('bhqk,bhkd->bhqd', attn, v)
        aT = adapter_wte.shape[0]
        prefix = adapter_wte[None]
        aqkv = jnp.einsum('btc,oc->bto', prefix, w_attn)
        _, ak, av = jnp.split(aqkv, 3, axis=-1)
        ak = ak.reshape(1, aT, H, hd).transpose(0, 2, 1, 3)
        av = av.reshape(1, aT, H, hd).transpose(0, 2, 1, 3)
        ascores = jnp.einsum('bhqd,xhkd->bhqk', q, ak) / jnp.sqrt(jnp.asarray(C, x.dtype))
        ascores = gating[0] * jax.nn.softmax(ascores.astype(jnp.float32), axis=-1).astype(q.dtype)
        y = y + jnp.einsum('bhqk,xhkd->bhqd', ascores, av)
        y = y.transpose(0, 2, 1, 3).reshape(B, T, C)
        return jnp.einsum('btc,oc->bto', y, w_proj)

    def _L0_cond2_ref(x, c, weight, c_weight, bias):
        import jax, jax.numpy as jnp
        import numpy as np
        from jax import lax
        N, C_IN, L = (32, 64, 1024)
        C_OUT, K, GROUPS = (64, 9, 4)
        C_DIM, PAD, STRIDE = (128, 4, 1)
        out = lax.conv_general_dilated(x, weight, window_strides=(STRIDE,), padding=[(PAD, PAD)], dimension_numbers=('NCH', 'OIH', 'NCH'), feature_group_count=GROUPS)
        ctx = jnp.einsum('nd,od->no', c, c_weight)
        out = out + ctx[:, :, None] + bias[None, :, None]
        return out

    def _L0_ffn_ref(x, W_base, b_base, W_router, A, B):
        import jax, jax.numpy as jnp
        import numpy as np
        NUM_EXPERTS = 8
        TOP_K = 2
        RANK = 16
        LORA_ALPHA = 32
        SCALING = LORA_ALPHA / RANK
        bs, seq, d_in = x.shape
        T = bs * seq
        xf = x.reshape(T, d_in)
        base = xf @ W_base.T + b_base
        logits = xf @ W_router.T
        rw, sel = jax.lax.top_k(logits, TOP_K)
        rw = jax.nn.softmax(rw, axis=-1)
        onehot = jax.nn.one_hot(sel, NUM_EXPERTS, dtype=rw.dtype)
        w = jnp.einsum('tk,tke->te', rw, onehot)
        h = jnp.einsum('td,erd->ter', xf, A)
        lora = jnp.einsum('ter,te,eor->to', h, w, B) * SCALING
        return (base + lora).reshape(bs, seq, -1)
    x = x + _L0_attn_ref(_L0_cond_ref(x, cond_128, L0_cond_W0, L0_cond_b0, L0_cond_W1, L0_cond_b1, L0_cond_W2, L0_cond_b2, L0_cond_weight, L0_cond_bias_k), L0_attn_w_attn, L0_attn_w_proj, L0_attn_adapter_wte, L0_attn_gating)
    x = x + _L0_ffn_ref(_L0_cond2_ref(x, cond_128, L0_cond2_weight, L0_cond2_c_weight, fside_S_0), L0_ffn_W_base, L0_ffn_b_base, L0_ffn_W_router, L0_ffn_A, L0_ffn_B)
    return x

_drawn_inputs = setup_inputs


def setup_inputs(seed=0):
    import zlib

    import numpy as np

    out = dict(_drawn_inputs(seed))
    spreads = {'L0_cond_b0': (0.0, 2.0), 'L0_cond_b1': (0.0, 0.8), 'L0_cond_b2': (0.0, 0.8)}
    factors = {'L0_cond_bias_k': 4.227, 'L0_ffn_b_base': 31.501}
    for name, (base, spread) in spreads.items():
        noise = np.random.default_rng([zlib.crc32(name.encode()), seed]).standard_normal(out[name].shape)
        drawn = base * np.exp(spread * noise) if base else spread * noise
        out[name] = jnp.asarray(drawn.astype(out[name].dtype))
    for name, factor in factors.items():
        out[name] = (out[name] * factor).astype(out[name].dtype)
    return out
```

```python
from contextlib import ExitStack

import numpy as np

import concourse.bass as bass
from concourse import mybir

F32 = mybir.dt.float32
F32R = mybir.dt.float32r
U32 = mybir.dt.uint32
ALU = mybir.AluOpType
ACT = mybir.ActivationFunctionType
AX = mybir.AxisListType.X
ds = bass.ds

P = 128
NB, NC, L = 32, 64, 1024
TOK = NB * NC
HD = 32
GH = P // HD
NG = L // P
UT = 512
NU = TOK // UT
UB = UT // NC
UP = UB // 2
KC = L // P
NP = NB // 2
NA = 10
NE, RANK = 8, 16
NM = 8
TAPS, CG = 9, 16
PH = 4
HC = 32
NF = L + NE * RANK + NE
SCALE = 1.0 / float(np.sqrt(HD))
ASCALE = 1.0 / float(np.sqrt(L))
LORA_SCALE = 32 / RANK
HALF_SWAP = [(i + HD // 2) % HD for i in range(HD)]
Q_, K_, V_ = 0, 1, 2
DMA_RING = 1024


def wait(eng, sem, value):
    if not isinstance(value, int) or value > 0:
        eng.wait_ge(sem, value)


def split_passes(hi_l, lo_l, hi_r, lo_r):
    return ((hi_l, hi_r), (hi_l, lo_r), (lo_l, hi_r))


def mix_phase(nc, d, bank, zhi, zlo, zhi_f):
    NX = 4
    with ExitStack() as ctx:
        def sb(name, shape, dt=F32):
            return ctx.enter_context(nc.sbuf_tensor(name, shape, dt))

        def sem(name):
            return ctx.enter_context(nc.semaphore(name))

        condT = sb("m_condT", [P, NB])
        w0 = sb("m_w0", [P, P])
        w1 = sb("m_w1", [P, P])
        w2 = sb("m_w2", [P, NM])
        b0 = sb("m_b0", [P, 1])
        b1 = sb("m_b1", [P, 1])
        b2 = sb("m_b2", [1, NM])
        ones = sb("m_ones", [1, NB])
        ident = sb("m_ident", [NB, NB])
        mixw = sb("m_mixw", [NM, NC, NC + 1])
        h0 = sb("m_h0", [P, NB])
        h1 = sb("m_h1", [P, NB])
        att = sb("m_att", [NB, NM])
        stat = sb("m_stat", [NB, 4])
        attT = sb("m_attT", [NM, NB])
        aggT = sb("m_aggT", [NC + 1, NB, NC])
        xbuf = [sb(f"m_x{j}", [NC + 1, L]) for j in range(NX)]

        consts = sem("m_consts")
        ones_set = sem("m_ones_set")
        mlp_mm = sem("m_mlp_mm")
        mlp_act = sem("m_mlp_act")
        soft = sem("m_soft")
        soft_exp = sem("m_soft_exp")
        att_tr = sem("m_att_tr")
        att_copied = sem("m_att_copied")
        agg_mm = sem("m_agg_mm")
        agg_copied = sem("m_agg_copied")
        x_in = [sem(f"m_x_in{j}") for j in range(NX)]
        z_mm = [sem(f"m_z_mm{j}") for j in range(NX)]
        z_hi = [sem(f"m_z_hi{j}") for j in range(NX)]
        z_lo = [sem(f"m_z_lo{j}") for j in range(NX)]
        NCONST = 9

        block = ctx.enter_context(nc.Block())

        @block.sync
        def _(sp):
            for dst, src in ((condT, "condT"), (w0, "W0"), (w1, "W1"), (w2, "W2"), (b0, "b0"), (b1, "b1"),
                             (b2, "b2"), (mixw, "mixw")):
                sp.dma_start(dst[:], d[src]).then_inc(consts, 16)
            sp.dma_start(ident[:], d["ident"][0:NB, 0:NB]).then_inc(consts, 16)
            for j in range(NX):
                sp.dma_start(xbuf[j][0:NC, :], d["x"][j]).then_inc(x_in[j], 16)
            with sp.Fori(1, NB // NX) as it:
                for j in range(NX):
                    sp.wait_ge(z_mm[j], it)
                    sp.dma_start(xbuf[j][0:NC, :], d["x"][ds(it * NX + j, 1)].rearrange("a c l -> (a c) l")
                                 ).then_inc(x_in[j], 16)

        @block.tensor
        def _(pe):
            pe.wait_ge(consts, 16 * NCONST)
            pe.wait_ge(ones_set, 1 + NX)
            pe.matmul(bank[0][:, 0:NB], w0[:], condT[:], start=True, stop=True).then_inc(mlp_mm, 1)
            pe.wait_ge(mlp_act, 1)
            pe.matmul(bank[0][:, 64:64 + NB], w1[:], h0[:], start=True, stop=True).then_inc(mlp_mm, 1)
            pe.wait_ge(mlp_act, 2)
            pe.matmul(bank[0][0:NB, 128:128 + NM], h1[:], w2[:], start=True, stop=False)
            pe.matmul(bank[0][0:NB, 128:128 + NM], ones[:], b2[:], start=False, stop=True).then_inc(mlp_mm, 1)
            pe.wait_ge(soft, 5)
            pe.transpose(bank[1][0:NM, 0:NB], att[:], ident[:]).then_inc(att_tr, 1)
            pe.wait_ge(att_copied, 1)
            for o in range(NC):
                mm = pe.matmul(bank[4 + o // 16][0:NC + 1, (o % 16) * NB:(o % 16 + 1) * NB], mixw[:, o, :], attT[:],
                               start=True, stop=True)
                if o % 16 == 15:
                    mm.then_inc(agg_mm, 1)
            pe.wait_ge(agg_copied, 4)
            with pe.Fori(0, NB // NX) as it:
                for j in range(NX):
                    pe.wait_ge(x_in[j], 16 * it + 16)
                    pe.wait_ge(z_lo[j], it)
                    for c in range(KC):
                        mm = pe.matmul(bank[j][:, c * NC:(c + 1) * NC], xbuf[j][:, c * P:(c + 1) * P],
                                       aggT[:, ds(it * NX + j, 1), :].rearrange("p a o -> p (a o)"),
                                       start=True, stop=True)
                    mm.then_inc(z_mm[j], 1)

        @block.scalar
        def _(act):
            for n, (h, b) in enumerate(((h0, b0), (h1, b1))):
                act.wait_ge(mlp_mm, n + 1)
                act.activation(h[:], bank[0][:, 64 * n:64 * n + NB], ACT.Gelu, bias=b[:, 0:1]).then_inc(mlp_act, 1)
            act.wait_ge(soft, 2)
            act.activation(att[:], att[:], ACT.Exp).then_inc(soft_exp, 1)
            for q in range(0, 4, 2):
                act.wait_ge(agg_mm, q + 1)
                act.activation(aggT[:, :, 16 * q:16 * q + 16].rearrange("p b o -> p o b"),
                               bank[4 + q][0:NC + 1, :].rearrange("p (o b) -> p o b", b=NB), ACT.Copy
                               ).then_inc(agg_copied, 1)
            with act.Fori(0, NB // NX) as it:
                for j in range(NX):
                    act.wait_ge(z_mm[j], it + 1)
                    act.activation(zhi[:, :, ds((it * NX + j) * NC, NC)],
                                   bank[j][:, :].rearrange("p (c t) -> p c t", t=NC), ACT.Copy).then_inc(z_hi[j], 1)

        @block.vector
        def _(dve):
            dve.memset(ones[:], 1.0).then_inc(ones_set, 1)
            for j in range(NX):
                dve.memset(xbuf[j][NC:NC + 1, :], 1.0).then_inc(ones_set, 1)
            dve.wait_ge(mlp_mm, 3)
            dve.reduce_max(stat[:, 0:1], bank[0][0:NB, 128:128 + NM], AX).then_inc(soft, 1)
            dve.wait_ge(soft, 1)
            dve.tensor_scalar(att[:], bank[0][0:NB, 128:128 + NM], stat[:, 0:1], None, ALU.subtract).then_inc(soft, 1)
            dve.wait_ge(soft_exp, 1)
            dve.reduce_sum(stat[:, 1:2], att[:], AX).then_inc(soft, 1)
            dve.wait_ge(soft, 3)
            dve.reciprocal(stat[:, 2:3], stat[:, 1:2]).then_inc(soft, 1)
            dve.wait_ge(soft, 4)
            dve.tensor_scalar(att[:], att[:], stat[:, 2:3], None, ALU.mult).then_inc(soft, 1)
            dve.wait_ge(att_tr, 1)
            dve.tensor_copy(attT[:], bank[1][0:NM, 0:NB]).then_inc(att_copied, 1)
            for q in range(1, 4, 2):
                dve.wait_ge(agg_mm, q + 1)
                dve.tensor_copy(aggT[:, :, 16 * q:16 * q + 16].rearrange("p b o -> p o b"),
                                bank[4 + q][0:NC + 1, :].rearrange("p (o b) -> p o b", b=NB)).then_inc(agg_copied, 1)
            with dve.Fori(0, NB // NX) as it:
                for j in range(NX):
                    dve.wait_ge(z_hi[j], it + 1)
                    cols = ds((it * NX + j) * NC, NC)
                    dve.tensor_tensor(zlo[:, :, cols], bank[j][:, :].rearrange("p (c t) -> p c t", t=NC),
                                      zhi_f[:, :, cols], ALU.subtract).then_inc(z_lo[j], 1)


def attention_phase(nc, d, bank, zhi, zlo, y_dram):
    with ExitStack() as ctx:
        def sb(name, shape, dt=F32):
            return ctx.enter_context(nc.sbuf_tensor(name, shape, dt))

        def sem(name):
            return ctx.enter_context(nc.semaphore(name))

        wst = sb("a_wst", [P, KC, 3, P])
        whi = sb("a_whi", [P, KC, 3, P], F32R)
        wlo = sb("a_wlo", [P, KC, 3, P], F32R)
        whi_f = whi[:, :, :, :].bitcast(F32)
        wte = sb("a_wte", [P, KC, NA])
        wtehi = sb("a_wtehi", [P, KC, P], F32R)
        wtelo = sb("a_wtelo", [P, KC, P], F32R)
        wtehi_f = wtehi[:, :, :].bitcast(F32)
        cosT = sb("a_cos", [P, NC])
        sinT = sb("a_sin", [P, NC])
        mask = sb("a_mask", [P, NC])
        ident = sb("a_ident", [P, P])
        gate = sb("a_gate", [P, 1])
        qr = sb("a_qr", [P, UT])
        kr = sb("a_kr", [P, UT])
        rot = sb("a_rot", [P, UT])
        kbd = sb("a_kbd", [P, UB, GH, NC])
        vT = sb("a_vT", [P, UT])
        vbd = sb("a_vbd", [P, UP, 2, 2, 2 * HD])
        prob = [sb(f"a_prob{t}", [P, 8, NC]) for t in range(2)]
        pT = [sb(f"a_pT{t}", [P, 2, 2, P]) for t in range(2)]
        stat = sb("a_stat", [P, 2, 3, 8])
        aprob = sb("a_aprob", [P, UP, GH, HD])
        atmp = sb("a_atmp", [P, UP * GH, NA])
        astat = sb("a_astat", [P, 3, UP * GH])
        aT = sb("a_aT", [P, UT])
        akv = sb("a_akv", [NA, 2 * P])
        akbd = sb("a_akbd", [P, GH, NA])
        avbd = sb("a_avbd", [P, P])
        ysb = sb("a_ysb", [P, UT])

        bS, bPT, bY, bAD, bQ, bK, bV = bank[0:2], bank[2], bank[3], bank[4], bank[5], bank[6], bank[7]
        AKT = 2 * P

        consts = sem("a_consts")
        cleared = sem("a_cleared")
        w_in = sem("a_w_in")
        wte_hi = sem("a_wte_hi")
        wte_lo = sem("a_wte_lo")
        w_hi = {Q_: sem("a_wq_hi"), K_: sem("a_wk_hi"), V_: sem("a_wv_hi")}
        w_lo = {Q_: sem("a_wq_lo"), K_: sem("a_wk_lo"), V_: sem("a_wv_lo")}
        mm_done = {Q_: sem("a_q_mm"), K_: sem("a_k_mm"), V_: sem("a_v_mm")}
        turned = {Q_: sem("a_q_turned"), K_: sem("a_k_turned")}
        rotated = {Q_: sem("a_q_rotated"), K_: sem("a_k_rotated")}
        rot_step = sem("a_rot_step")
        kbd_set = sem("a_kbd_set")
        vT_copied = sem("a_vT_copied")
        v_tr = sem("a_v_tr")
        vbd_set = sem("a_vbd_set")
        scores = sem("a_scores")
        masked = sem("a_masked")
        row_max = sem("a_row_max")
        shifted = sem("a_shifted")
        exped = sem("a_exped")
        row_sum = sem("a_row_sum")
        inverted = sem("a_inverted")
        probs = sem("a_probs")
        p_tr = sem("a_p_tr")
        pT_copied = sem("a_pT_copied")
        ascores = sem("a_ascores")
        amax = sem("a_amax")
        ashifted = sem("a_ashifted")
        aexped = sem("a_aexped")
        asum = sem("a_asum")
        ainv = sem("a_ainv")
        agated = sem("a_agated")
        aprobs = sem("a_aprobs")
        a_tr = sem("a_a_tr")
        aT_copied = sem("a_aT_copied")
        akv_mm = sem("a_akv_mm")
        akv_copied = sem("a_akv_copied")
        ak_tr = sem("a_ak_tr")
        akbd_set = sem("a_akbd_set")
        avbd_set = sem("a_avbd_set")
        y_mm = sem("a_y_mm")
        y_copied = sem("a_y_copied")
        y_out = sem("a_y_out")
        NCONST, NCLEAR = 6, 7

        block = ctx.enter_context(nc.Block())

        def phases(eng, step, tail):
            step(0, 0)
            with eng.Fori(0, NG - 1) as g:
                for u in range(1, NU):
                    step(g, u)
                step(g + 1, 0)
            for u in range(1, NU):
                step(NG - 1, u)
            tail()

        def first(g, u):
            return isinstance(g, int) and g == 0 and u == 0

        def refill(g, u):
            return u == NU - 1 and not (isinstance(g, int) and g == NG - 1)

        @block.sync
        def _(sp):
            for dst, src in ((wte, "wteT"), (cosT, "cos"), (sinT, "sin"), (mask, "mask"), (ident, "ident"),
                             (gate, "gate")):
                sp.dma_start(dst[:], d[src]).then_inc(consts, 16)
            sp.dma_start(wst[:], d["wqkvT"][0]).then_inc(w_in, 16)

            def store(g, u):
                sp.wait_ge(y_copied, NU * g + u + 1)
                sp.dma_start(y_dram[u * UP:(u + 1) * UP, :, ds(g, 1), :].rearrange("i p a t -> p i (a t)"),
                             ysb[:].rearrange("p (i t) -> p i t", i=UP)).then_inc(y_out, 16)

            def step(g, u):
                if u == 0 and not (isinstance(g, int) and g == NG - 1):
                    pass
                if not first(g, u):
                    store(*((g, u - 1) if u else (g - 1, NU - 1)))
                if u == 1 and not (isinstance(g, int) and g == NG - 1):
                    for x in (Q_, K_, V_):
                        sp.wait_ge(w_lo[x], g + 1)
                    sp.dma_start(wst[:], d["wqkvT"][ds(g + 1, 1)].rearrange("a p k x c -> p (a k) x c")
                                 ).then_inc(w_in, 16)

            def tail():
                store(NG - 1, NU - 1)
                sp.wait_ge(y_out, 16 * NG * NU)

            phases(sp, step, tail)

        @block.gpsimd
        def _(pool):
            for t in (kbd, vbd, aprob, avbd, akbd):
                pool.memset(t[:], 0.0).then_inc(cleared, 1)
            for t in (wtehi, wtelo):
                pool.memset(t[:].bitcast(F32), 0.0).then_inc(cleared, 1)

        @block.tensor
        def _(pe):
            pe.wait_ge(consts, 16 * NCONST)
            pe.wait_ge(wte_lo, 1)

            def attend_scores(m):
                pe.wait_ge(rotated[Q_], m + 1)
                pe.wait_ge(kbd_set, m + 1)
                wait(pe, aT_copied, m)
                wait(pe, pT_copied, 2 * m)
                for s in range(UP):
                    for b in range(2):
                        mm = pe.matmul(bS[s // 2][NC * b:NC * b + NC, (s % 2) * GH * NC:(s % 2 + 1) * GH * NC],
                                       qr[:, (2 * s + b) * NC:(2 * s + b + 1) * NC],
                                       kbd[:, 2 * s + b, :, :].rearrange("p h k -> p (h k)"), start=True, stop=True)
                    if s % 2:
                        mm.then_inc(scores, 1)

            def attend_ascores(m, groups):
                wait(pe, ashifted, m)
                pe.wait_ge(akbd_set, groups)
                for i in range(UP):
                    mm = pe.matmul(bAD[:, i * GH * NA:(i + 1) * GH * NA], qr[:, i * P:(i + 1) * P],
                                   akbd[:].rearrange("p h a -> p (h a)"), start=True, stop=True)
                mm.then_inc(ascores, 1)

            def attend_transposes(m):
                pe.wait_ge(aprobs, m + 1)
                for i in range(UP):
                    tr = pe.transpose(bS[0][:, i * P:(i + 1) * P], aprob[:, i, :, :].rearrange("p h a -> p (h a)"),
                                      ident[:])
                tr.then_inc(a_tr, 1)
                wait(pe, pT_copied, 2 * m)
                for t, dst in ((0, bPT), (1, bS[1])):
                    pe.wait_ge(probs, 2 * m + t + 1)
                    for j in range(4):
                        tr = pe.transpose(dst[:, j * P:(j + 1) * P],
                                          prob[t][:, 2 * j:2 * j + 2, :].rearrange("p h k -> p (h k)"), ident[:])
                    tr.then_inc(p_tr, 1)

            def attend_values(m, groups):
                pe.wait_ge(aT_copied, m + 1)
                pe.wait_ge(avbd_set, groups)
                wait(pe, y_copied, m)
                pe.matmul(bY[:], avbd[:], aT[:], start=True, stop=True)
                pe.wait_ge(vbd_set, m + 1)
                for s in range(UP):
                    if s % 2 == 0:
                        pe.wait_ge(pT_copied, 2 * m + s // 2 + 1)
                    for b in range(2):
                        for hp in range(2):
                            mm = pe.matmul(bY[2 * HD * hp:2 * HD * (hp + 1), (2 * s + b) * NC:(2 * s + b + 1) * NC],
                                           vbd[:, s, b, hp, :], pT[s // 2][:, s % 2, hp, NC * b:NC * b + NC],
                                           start=False, stop=True, skip_group_check=True)
                mm.then_inc(y_mm, 1)

            def project(x, dst, g, u):
                pe.wait_ge(w_lo[x], g + 1)
                for c in range(KC):
                    for i, (w, z) in enumerate(split_passes(whi, wlo, zhi, zlo)):
                        mm = pe.matmul(dst[:], w[:, c, x, :], z[:, c, u * UT:(u + 1) * UT],
                                       start=(c == 0 and i == 0), stop=(c == KC - 1 and i == 2))
                mm.then_inc(mm_done[x], 1)

            def step(g, u):
                n = NU * g + u
                groups = g + 1 if u else g
                att = not first(g, u)
                if att:
                    attend_scores(n - 1)
                    attend_ascores(n - 1, groups)
                wait(pe, turned[K_], n)
                project(K_, bK, g, u)
                wait(pe, turned[Q_], n)
                project(Q_, bQ, g, u)
                if att:
                    attend_transposes(n - 1)
                wait(pe, vbd_set, n)
                project(V_, bV, g, u)
                if u == 0:
                    wait(pe, ashifted, n)
                    for c in range(KC):
                        for i, (a, w) in enumerate(split_passes(wtehi, wtelo, whi, wlo)):
                            mm = pe.matmul(bAD[:, 0:2 * P], a[:, c, :], w[:, c, K_:V_ + 1, :].rearrange("p x c -> p (x c)"),
                                           start=(c == 0 and i == 0), stop=(c == KC - 1 and i == 2))
                    mm.then_inc(akv_mm, 1)
                if att:
                    attend_values(n - 1, groups)
                if u == 0:
                    pe.wait_ge(akv_copied, g + 1)
                pe.wait_ge(vT_copied, n + 1)
                for i in range(UP):
                    tr = pe.transpose(bV[:, i * P:(i + 1) * P], vT[:, i * P:(i + 1) * P], ident[:])
                tr.then_inc(v_tr, 1)
                if u == 0:
                    pe.transpose(bAD[:, AKT:AKT + NA], akv[:, 0:P], ident[0:NA, 0:NA]).then_inc(ak_tr, 1)

            def tail():
                m = NG * NU - 1
                attend_scores(m)
                attend_ascores(m, NG)
                attend_transposes(m)
                attend_values(m, NG)

            phases(pe, step, tail)

        @block.scalar
        def _(act):
            act.wait_ge(consts, 16 * NCONST)
            act.wait_ge(cleared, NCLEAR)
            act.activation(wtehi[:, :, 0:NA], wte[:], ACT.Copy).then_inc(wte_hi, 1)

            def split_hi(x, g, n):
                act.wait_ge(w_in, 16 * g + 16)
                wait(act, mm_done[x], n)
                if x != Q_:
                    wait(act, akv_mm, g)
                act.activation(whi[:, :, x, :], wst[:, :, x, :], ACT.Copy).then_inc(w_hi[x], 1)

            def attend_exp(m):
                for t in range(2):
                    act.wait_ge(shifted, 2 * m + t + 1)
                    act.activation(prob[t][:], prob[t][:], ACT.Exp, scale=SCALE).then_inc(exped, 1)
                act.wait_ge(ashifted, m + 1)
                act.activation(atmp[:], atmp[:], ACT.Exp, scale=ASCALE).then_inc(aexped, 1)

            def attend_copies(m):
                act.wait_ge(a_tr, m + 1)
                wait(act, y_mm, m)
                act.activation(aT[:], bS[0][:], ACT.Copy).then_inc(aT_copied, 1)
                for t, src in ((0, bPT), (1, bS[1])):
                    act.wait_ge(p_tr, 2 * m + t + 1)
                    act.activation(pT[t][:].rearrange("p s h q -> p (s h q)"), src[:], ACT.Copy).then_inc(pT_copied, 1)

            def y_copy(m):
                act.wait_ge(y_mm, m + 1)
                wait(act, y_out, 16 * m)
                act.activation(ysb[:], bY[:], ACT.Copy).then_inc(y_copied, 1)

            def step(g, u):
                n = NU * g + u
                att = not first(g, u)
                if att:
                    attend_exp(n - 1)
                act.wait_ge(rotated[K_], n + 1)
                wait(act, scores, 2 * n)
                for h in range(GH):
                    cp = act.activation(kbd[HD * h:HD * (h + 1), :, h, :],
                                        kr[HD * h:HD * (h + 1), :].rearrange("p (b k) -> p b k", k=NC), ACT.Copy)
                cp.then_inc(kbd_set, 1)
                if refill(g, u):
                    split_hi(K_, g + 1, n + 1)
                if att:
                    attend_copies(n - 1)
                if refill(g, u):
                    split_hi(Q_, g + 1, n + 1)
                act.wait_ge(mm_done[V_], n + 1)
                wait(act, v_tr, n)
                act.activation(vT[:], bV[:], ACT.Copy).then_inc(vT_copied, 1)
                if refill(g, u):
                    split_hi(V_, g + 1, n + 1)
                if u == 0:
                    act.wait_ge(akv_mm, g + 1)
                    wait(act, avbd_set, g)
                    wait(act, ak_tr, g)
                    act.activation(akv[:], bAD[0:NA, 0:2 * P], ACT.Copy).then_inc(akv_copied, 1)
                if att:
                    y_copy(n - 1)
                if u == 0:
                    act.wait_ge(akv_copied, g + 1)
                    wait(act, y_mm, n)
                    for h in range(GH):
                        cp = act.activation(avbd[HD * h:HD * h + NA, HD * h:HD * (h + 1)],
                                            akv[:, P + HD * h:P + HD * (h + 1)], ACT.Copy)
                    cp.then_inc(avbd_set, 1)
                    act.wait_ge(ak_tr, g + 1)
                    wait(act, ascores, n)
                    for h in range(GH):
                        cp = act.activation(akbd[HD * h:HD * (h + 1), h, :], bAD[HD * h:HD * (h + 1), AKT:AKT + NA],
                                            ACT.Copy)
                    cp.then_inc(akbd_set, 1)
                act.wait_ge(v_tr, n + 1)
                wait(act, y_mm, n)
                for b in range(2):
                    for h in range(2):
                        cp = act.activation(
                            vbd[NC * h:NC * (h + 1), :, b, :, HD * h:HD * (h + 1)],
                            bV[NC * b:NC * (b + 1), :].rearrange("p (s a h e) -> p s a h e", s=UP, a=2, h=2)[:, :, :, h, :],
                            ACT.Copy)
                cp.then_inc(vbd_set, 1)

            def tail():
                m = NG * NU - 1
                attend_exp(m)
                attend_copies(m)
                y_copy(m)

            for x in (K_, Q_, V_):
                split_hi(x, 0, 0)
            phases(act, step, tail)

        @block.vector
        def _(dve):
            dve.wait_ge(wte_hi, 1)
            dve.tensor_tensor(wtelo[:, :, 0:NA], wte[:], wtehi_f[:, :, 0:NA], ALU.subtract).then_inc(wte_lo, 1)

            def split_lo(x, g, n):
                dve.wait_ge(w_hi[x], g + 1)
                wait(dve, mm_done[x], n)
                if x != Q_:
                    wait(dve, akv_mm, g)
                dve.tensor_tensor(wlo[:, :, x, :], wst[:, :, x, :], whi_f[:, :, x, :], ALU.subtract
                                  ).then_inc(w_lo[x], 1)

            def rotate(x, src, dst, n, used, count):
                tab = [t[:].rearrange("p (a k) -> p a k", a=1).broadcast_to([P, UB, NC]) for t in (cosT, sinT)]
                i = 0 if x == K_ else 2
                dve.wait_ge(mm_done[x], n + 1)
                wait(dve, rotated[Q_ if x == K_ else K_], n if x == K_ else n + 1)
                for s, c in used:
                    wait(dve, s, c)
                dve.tensor_tensor(dst[:].rearrange("p (b k) -> p b k", k=NC),
                                  src[:].rearrange("p (b k) -> p b k", k=NC), tab[0], ALU.mult).then_inc(rot_step, 1)
                dve.stream_shuffle(rot[:], src[:], HALF_SWAP).then_inc(turned[x], 1)
                dve.wait_ge(turned[x], n + 1)
                r = rot[:].rearrange("p (b k) -> p b k", k=NC)
                dve.tensor_tensor(r, r, tab[1], ALU.mult).then_inc(rot_step, 1)
                dve.wait_ge(rot_step, 4 * n + i + 2)
                dve.tensor_tensor(dst[:], dst[:], rot[:], ALU.add).then_inc(rotated[x], 1)

            def attend_softmax(m):
                maskb = mask[:].rearrange("p (a k) -> p a k", a=1).broadcast_to([P, 8, NC])

                def spread(t, k):
                    return stat[:, t, k, :].rearrange("p (a b) -> p a b", b=1).broadcast_to([P, 8, NC])

                def aspread(k):
                    return astat[:, k, :].rearrange("p (a b) -> p a b", b=1).broadcast_to([P, UP * GH, NA])

                for t in range(2):
                    dve.wait_ge(scores, 2 * m + t + 1)
                    wait(dve, p_tr, 2 * m)
                    dve.tensor_tensor(prob[t][:], bS[t][:].rearrange("p (a k) -> p a k", k=NC), maskb, ALU.add
                                      ).then_inc(masked, 1)
                    dve.wait_ge(masked, 2 * m + t + 1)
                    dve.tensor_reduce(stat[:, t, 0, :], prob[t][:], AX, ALU.max).then_inc(row_max, 1)
                    dve.wait_ge(row_max, 2 * m + t + 1)
                    dve.tensor_tensor(prob[t][:], prob[t][:], spread(t, 0), ALU.subtract).then_inc(shifted, 1)
                dve.wait_ge(ascores, m + 1)
                asrc = bAD[:, 0:UP * GH * NA].rearrange("p (a k) -> p a k", k=NA)
                dve.tensor_reduce(astat[:, 0, :], asrc, AX, ALU.max).then_inc(amax, 1)
                dve.wait_ge(amax, m + 1)
                wait(dve, aprobs, m)
                dve.tensor_tensor(atmp[:], asrc, aspread(0), ALU.subtract).then_inc(ashifted, 1)
                for t in range(2):
                    dve.wait_ge(exped, 2 * m + t + 1)
                    dve.tensor_reduce(stat[:, t, 1, :], prob[t][:], AX, ALU.add).then_inc(row_sum, 1)
                    dve.wait_ge(row_sum, 2 * m + t + 1)
                    dve.reciprocal(stat[:, t, 2, :], stat[:, t, 1, :]).then_inc(inverted, 1)
                    dve.wait_ge(inverted, 2 * m + t + 1)
                    dve.tensor_tensor(prob[t][:], prob[t][:], spread(t, 2), ALU.mult).then_inc(probs, 1)
                dve.wait_ge(aexped, m + 1)
                dve.tensor_reduce(astat[:, 1, :], atmp[:], AX, ALU.add).then_inc(asum, 1)
                dve.wait_ge(asum, m + 1)
                dve.reciprocal(astat[:, 2, :], astat[:, 1, :]).then_inc(ainv, 1)
                dve.wait_ge(ainv, m + 1)
                dve.tensor_scalar(astat[:, 2, :], astat[:, 2, :], gate[:, 0:1], None, ALU.mult).then_inc(agated, 1)
                dve.wait_ge(agated, m + 1)
                wait(dve, a_tr, m)
                dve.tensor_tensor(aprob[:].rearrange("p i h a -> p (i h) a")[:, :, 0:NA], atmp[:], aspread(2), ALU.mult
                                  ).then_inc(aprobs, 1)

            def step(g, u):
                n = NU * g + u
                if not first(g, u):
                    attend_softmax(n - 1)
                rotate(K_, bK, kr, n, ((kbd_set, n),), n)
                if refill(g, u):
                    split_lo(K_, g + 1, n + 1)
                rotate(Q_, bQ, qr, n, ((scores, 2 * n), (ascores, n)), n)
                if refill(g, u):
                    split_lo(Q_, g + 1, n + 1)
                    split_lo(V_, g + 1, n + 1)

            for x in (K_, Q_, V_):
                split_lo(x, 0, 0)
            phases(dve, step, lambda: attend_softmax(NG * NU - 1))


def ffn_phase(nc, d, bank2, y_dram, out):
    with ExitStack() as ctx:
        def sb(name, shape, dt=F32):
            return ctx.enter_context(nc.sbuf_tensor(name, shape, dt))

        def sem(name):
            return ctx.enter_context(nc.semaphore(name))

        bP, bF, bC, bMisc = bank2
        bR = bMisc[:, 0:512]
        bT = bMisc[:, 512:1024]

        wphi = sb("f_wphi", [P, KC, L], F32R)
        wplo = sb("f_wplo", [P, KC, L], F32R)
        wfhi = sb("f_wfhi", [P, KC, NF], F32R)
        wflo = sb("f_wflo", [P, KC, NF], F32R)
        NST = 3
        loraB = sb("f_loraB", [P, L])
        toep = sb("f_toep", [P, 6, P])
        ctxb = sb("f_ctxb", [P, TOK])
        bbase = sb("f_bbase", [P, L])
        ident = sb("f_ident", [P, P])
        iota = sb("f_iota", [P, NE])
        condT = sb("f_condT", [P, NB])
        cwT = sb("f_cwT", [P, NC])
        fside = sb("f_fside", [P, NC])
        ones = sb("f_ones", [P, P])
        yst = sb("f_yst", [P, KC, P])
        yhi = sb("f_yhi", [P, KC, P], F32R)
        ylo = sb("f_ylo", [P, KC, P], F32R)
        xt = sb("f_xt", [P, L])
        x1 = sb("f_x1", [P, L])
        x1b = sb("f_x1b", [P, L])
        XW = PH + L + PH
        x4 = sb("f_x4", [P, 2, 2, XW])
        wst = [x4[:].rearrange("p b h t -> p (b h t)")[:, i * NF:(i + 1) * NF] for i in range(NST)]
        ct = sb("f_ct", [P, KC, P])
        chi = sb("f_chi", [P, KC, P], F32R)
        clo = sb("f_clo", [P, KC, P], F32R)
        osb = sb("f_osb", [P, L])
        lg = sb("f_lg", [P, NE])
        top = sb("f_top", [P, 8])
        topi = sb("f_topi", [P, 8], U32)
        rs = sb("f_rs", [P, 8])
        we = sb("f_we", [P, 3, NE])
        hw = sb("f_hw", [P, P])
        hwT = sb("f_hwT", [P, P])

        consts = sem("f_consts")
        cleared = sem("f_cleared")
        w_in = [sem(f"f_w_in{i}") for i in range(NST)]
        w_hi = sem("f_w_hi")
        w_lo = sem("f_w_lo")
        prods = sem("f_prods")
        ctx_mm = sem("f_ctx_mm")
        ctx_set = sem("f_ctx_set")
        y_in = sem("f_y_in")
        y_hi = sem("f_y_hi")
        y_lo = sem("f_y_lo")
        x_in = sem("f_x_in")
        proj_mm = sem("f_proj_mm")
        x1_set = sem("f_x1_set")
        x1b_set = sem("f_x1b_set")
        x4_in = sem("f_x4_in")
        conv_mm = sem("f_conv_mm")
        conv_set = sem("f_conv_set")
        c_hi = sem("f_c_hi")
        c_lo = sem("f_c_lo")
        ffn_mm = sem("f_ffn_mm")
        route = sem("f_route")
        route_exp = sem("f_route_exp")
        hw_set = sem("f_hw_set")
        hw_tr = sem("f_hw_tr")
        hwT_set = sem("f_hwT_set")
        lora_mm = sem("f_lora_mm")
        out_set = sem("f_out_set")
        stored = sem("f_stored")
        NCONST = 8
        NX4 = 16
        weights = [("wprojT", c, wphi, wplo, L) for c in range(KC)] + [("wffnT", c, wfhi, wflo, NF) for c in range(KC)]
        NW = len(weights)

        block = ctx.enter_context(nc.Block())

        def phases(eng, head, step, last):
            head()
            with eng.Fori(0, NP - 2) as p:
                step(p)
            step(NP - 2)
            last()

        def more(p):
            return not isinstance(p, int) or p < NP - 2

        @block.sync
        def _(sp):
            def load_w(i):
                name, c, _, _, n = weights[i]
                wait(sp, w_lo, i - NST + 1)
                sp.dma_start(wst[i % NST][:, 0:n], d[name][c]).then_inc(w_in[i % NST], 16)

            def load_y(p):
                wait(sp, y_lo, p)
                sp.dma_start(yst[:], y_dram[ds(p, 1)].rearrange("a p k t -> p (a k) t")).then_inc(y_in, 16)

            def load_x(p):
                wait(sp, x1_set, p)
                sp.dma_start(xt[:], d["x"][ds(p * 2, 2)].rearrange("b c l -> (b c) l")).then_inc(x_in, 16)

            def spread(p):
                sp.wait_ge(x1_set, p + 1)
                wait(sp, conv_mm, 2 * p)
                if isinstance(p, int) and p == 0:
                    sp.wait_ge(w_lo, NW)
                for b in range(2):
                    for h in range(2):
                        for f in range(PH):
                            r = b * NC + h * HC
                            sp.dma_start(x4[HC * f:HC * (f + 1), b, h, PH - f:PH - f + L], x1[r:r + HC, :]
                                         ).then_inc(x4_in, 16)

            def store(p):
                sp.wait_ge(out_set, p + 1)
                sp.dma_start(out[ds(p * 2, 2)].rearrange("b c l -> (b c) l"), osb[:]).then_inc(stored, 16)

            for i in range(NST):
                load_w(i)
            load_y(0)
            load_x(0)
            for dst, src in ((loraB, "loraB"), (toep, "toep"), (bbase, "bbase"), (ident, "ident"), (iota, "iota"),
                             (condT, "condT"), (cwT, "cwT"), (fside, "fside")):
                sp.dma_start(dst[:], d[src]).then_inc(consts, 16)
            for i in range(NST, NW):
                load_w(i)

            def head():
                spread(0)
                load_x(1)
                load_y(1)

            def step(p):
                spread(p + 1)
                if more(p):
                    load_x(p + 2)
                    load_y(p + 2)
                store(p)

            def last():
                store(NP - 1)
                sp.wait_ge(stored, 16 * NP)

            phases(sp, head, step, last)

        @block.gpsimd
        def _(pool):
            pool.memset(ones[:], 1.0).then_inc(cleared, 1)
            pool.wait_ge(w_lo, NW)
            pool.memset(x4[:, :, :, 0:1], 0.0).then_inc(cleared, 1)
            pool.memset(x4[:, :, :, PH + L:PH + L + 1], 0.0).then_inc(cleared, 1)
            pool.wait_ge(consts, 16 * NCONST)

            def add_bias(p):
                pool.wait_ge(x1_set, p + 1)
                wait(pool, out_set, p)
                pool.tensor_tensor(x1b[:], x1[:], bbase[:], ALU.add).then_inc(x1b_set, 1)

            phases(pool, lambda: add_bias(0), lambda p: add_bias(p + 1), lambda: None)

        @block.tensor
        def _(pe):
            pe.wait_ge(cleared, 1)
            pe.wait_ge(consts, 16 * NCONST)
            for i in range(TOK // 512):
                pe.wait_ge(prods, i + 1)
                wait(pe, ctx_set, i - 1)
                pe.matmul(bMisc[:, (i % 2) * 512:(i % 2 + 1) * 512], ones[:], osb[:, (i % 2) * 512:(i % 2 + 1) * 512],
                          start=True, stop=True).then_inc(ctx_mm, 1)

            def project(p, head=False):
                pe.wait_ge(y_lo, p + 1)
                wait(pe, x1_set, p)
                for c in range(KC):
                    if head:
                        pe.wait_ge(w_lo, c + 1)
                    for i, (y, w) in enumerate(split_passes(yhi, ylo, wphi, wplo)):
                        for n in range(2):
                            mm = pe.matmul(bP[:, n * 512:(n + 1) * 512], y[:, c, :], w[:, c, n * 512:(n + 1) * 512],
                                           start=(c == 0 and i == 0), stop=(c == KC - 1 and i == 2))
                mm.then_inc(proj_mm, 1)

            def convolve(p):
                pe.wait_ge(x4_in, 16 * NX4 * (p + 1))
                wait(pe, conv_set, 2 * p)
                for k in range(2):
                    for b in range(2):
                        for h in range(2):
                            for j in range(3):
                                t = PH * (P * k + j)
                                o = (2 * k + b) * 256 + h * P
                                mm = pe.matmul(bC[:, o:o + P], x4[:, b, h, t:t + PH * (P - 1) + 1:PH],
                                               toep[:, 3 * h + j, :], start=(j == 0), stop=(j == 2))
                    mm.then_inc(conv_mm, 1)

            def last_layer(p, head=False):
                pe.wait_ge(c_lo, p + 1)
                wait(pe, out_set, p)
                wait(pe, hw_set, p)
                for c in range(KC):
                    for i, (a, w) in enumerate(split_passes(chi, clo, wfhi, wflo)):
                        for dst, n0, n1 in ((bF[:, 0:512], 0, 512), (bF[:, 512:1024], 512, 1024),
                                            (bR[:, 0:NF - L], L, NF)):
                            mm = pe.matmul(dst, a[:, c, :], w[:, c, n0:n1], start=(c == 0 and i == 0),
                                           stop=(c == KC - 1 and i == 2))
                mm.then_inc(ffn_mm, 1)

            def low_rank(p):
                pe.wait_ge(hw_set, p + 1)
                wait(pe, hwT_set, p)
                pe.transpose(bT[:, 0:P], hw[:], ident[:]).then_inc(hw_tr, 1)
                pe.wait_ge(hwT_set, p + 1)
                for n in range(2):
                    mm = pe.matmul(bF[:, n * 512:(n + 1) * 512], hwT[:], loraB[:, n * 512:(n + 1) * 512],
                                   start=False, stop=True, skip_group_check=True)
                mm.then_inc(lora_mm, 1)

            def head():
                project(0, head=True)
                pe.wait_ge(cleared, 3)
                convolve(0)
                pe.wait_ge(w_lo, NW)

            def step(p):
                project(p + 1)
                last_layer(p)
                convolve(p + 1)
                low_rank(p)

            def last():
                last_layer(NP - 1)
                low_rank(NP - 1)

            phases(pe, head, step, last)

        @block.scalar
        def _(act):
            def split_y(p):
                act.wait_ge(y_in, 16 * (p + 1))
                wait(act, proj_mm, p)
                act.activation(yhi[:], yst[:], ACT.Copy).then_inc(y_hi, 1)

            def split_conv(p):
                act.wait_ge(conv_set, 2 * (p + 1))
                wait(act, ffn_mm, p)
                act.activation(chi[:], ct[:], ACT.Copy).then_inc(c_hi, 1)

            def route_and_copy(p):
                act.wait_ge(route, ROUTE_EXP + ROUTE_ALL * p)
                act.activation(rs[:, 1:2], rs[:, 0:1], ACT.Exp).then_inc(route_exp, 1)
                act.wait_ge(hw_tr, p + 1)
                wait(act, lora_mm, p)
                act.activation(hwT[:], bT[:, 0:P], ACT.Copy).then_inc(hwT_set, 1)

            for i, (_, c, hi, _, n) in enumerate(weights):
                act.wait_ge(w_in[i % NST], 16 * (i // NST + 1))
                act.activation(hi[:, c, :], wst[i % NST][:, 0:n], ACT.Copy).then_inc(w_hi, 1)
                if i == 0:
                    split_y(0)

            def head():
                split_y(1)
                split_conv(0)

            def step(p):
                if more(p):
                    split_y(p + 2)
                route_and_copy(p)
                split_conv(p + 1)

            phases(act, head, step, lambda: route_and_copy(NP - 1))

        @block.vector
        def _(dve):
            def split_y(p):
                dve.wait_ge(y_hi, p + 1)
                wait(dve, proj_mm, p)
                dve.tensor_tensor(ylo[:], yst[:], yhi[:].bitcast(F32), ALU.subtract).then_inc(y_lo, 1)

            def residual(p):
                dve.wait_ge(proj_mm, p + 1)
                dve.wait_ge(x_in, 16 * (p + 1))
                wait(dve, x1b_set, p)
                wait(dve, x4_in, 16 * NX4 * p)
                dve.tensor_tensor(x1[:], bP[:], xt[:], ALU.add).then_inc(x1_set, 1)

            def add_context(p):
                wait(dve, c_lo, p)
                for k in range(2):
                    dve.wait_ge(conv_mm, 2 * p + k + 1)
                    for b in range(2):
                        o = (2 * k + b) * 256
                        bias = ctxb[:, ds(p * P + b * NC, NC)].rearrange("p (h a o) -> p h a o", h=2, a=1)
                        for h in range(2):
                            op = dve.tensor_tensor(
                                ct[:, PH * k:PH * (k + 1), b * NC + h * HC:b * NC + (h + 1) * HC],
                                bC[:, o + h * P:o + (h + 1) * P].rearrange("p (q o) -> p q o", q=PH),
                                bias[:, h, :, :].broadcast_to([P, PH, HC]), ALU.add)
                    op.then_inc(conv_set, 1)

            def split_conv(p):
                dve.wait_ge(c_hi, p + 1)
                wait(dve, ffn_mm, p)
                dve.tensor_tensor(clo[:], ct[:], chi[:].bitcast(F32), ALU.subtract).then_inc(c_lo, 1)

            def router(p):
                base = ROUTE_ALL * p
                count = [0]

                def then(ins):
                    ins.then_inc(route, 1)
                    count[0] += 1
                    dve.wait_ge(route, base + count[0])

                dve.wait_ge(ffn_mm, p + 1)
                dve.tensor_copy(lg[:], bR[:, P:P + NE]).then_inc(route, 1)
                count[0] += 1
                then(dve.max(top[:], bR[:, P:P + NE]))
                dve.tensor_tensor(rs[:, 0:1], top[:, 1:2], top[:, 0:1], ALU.subtract).then_inc(route, 1)
                count[0] += 1
                assert count[0] == ROUTE_EXP
                then(dve.max_index(topi[:], top[:], lg[:]))
                then(dve.tensor_copy(rs[:, 4:6], topi[:, 0:2]))
                dve.wait_ge(route_exp, p + 1)
                then(dve.tensor_scalar(rs[:, 2:3], rs[:, 1:2], 1.0, None, ALU.add))
                then(dve.reciprocal(rs[:, 3:4], rs[:, 2:3]))
                then(dve.tensor_scalar(rs[:, 6:7], rs[:, 3:4], LORA_SCALE, None, ALU.mult))
                then(dve.tensor_tensor(rs[:, 7:8], rs[:, 1:2], rs[:, 6:7], ALU.mult))
                for k in range(2):
                    then(dve.tensor_scalar(we[:, k, :], iota[:], rs[:, 4 + k:5 + k], rs[:, 6 + k:7 + k],
                                           ALU.is_equal, ALU.mult))
                then(dve.tensor_tensor(we[:, 2, :], we[:, 0, :], we[:, 1, :], ALU.add))
                assert count[0] == ROUTE_ALL
                wait(dve, hw_tr, p)
                dve.tensor_tensor(hw[:].rearrange("p (e r) -> p e r", r=RANK),
                                  bR[:, 0:P].rearrange("p (e r) -> p e r", r=RANK),
                                  we[:, 2, :].rearrange("p (e a) -> p e a", a=1).broadcast_to([P, NE, RANK]),
                                  ALU.mult).then_inc(hw_set, 1)

            def finish(p):
                dve.wait_ge(lora_mm, p + 1)
                dve.wait_ge(x1b_set, p + 1)
                wait(dve, stored, 16 * p)
                dve.tensor_tensor(osb[:], bF[:], x1b[:], ALU.add).then_inc(out_set, 1)

            dve.wait_ge(consts, 16 * NCONST)
            for i in range(TOK // 512):
                cols = osb[:, (i % 2) * 512:(i % 2 + 1) * 512].rearrange("p (b o) -> p b o", o=NC)
                wait(dve, ctx_mm, i - 1)
                dve.tensor_tensor(cols, condT[:, 8 * i:8 * i + 8].rearrange("p (b a) -> p b a", a=1).broadcast_to([P, 8, NC]),
                                  cwT[:].rearrange("p (a o) -> p a o", a=1).broadcast_to([P, 8, NC]), ALU.mult
                                  ).then_inc(prods, 1)
                dve.wait_ge(ctx_mm, i + 1)
                dve.tensor_tensor(ctxb[:, 512 * i:512 * (i + 1)].rearrange("p (b o) -> p b o", o=NC),
                                  bMisc[:, (i % 2) * 512:(i % 2 + 1) * 512].rearrange("p (b o) -> p b o", o=NC),
                                  fside[:].rearrange("p (a o) -> p a o", a=1).broadcast_to([P, 8, NC]), ALU.add
                                  ).then_inc(ctx_set, 1)
            for i, (_, c, hi, lo, n) in enumerate(weights):
                dve.wait_ge(w_hi, i + 1)
                dve.tensor_tensor(lo[:, c, :], wst[i % NST][:, 0:n], hi[:, c, :].bitcast(F32), ALU.subtract
                                  ).then_inc(w_lo, 1)
                if i == 0:
                    split_y(0)
            dve.wait_ge(ctx_set, TOK // 512)

            def head():
                residual(0)
                split_y(1)
                add_context(0)
                split_conv(0)

            def step(p):
                residual(p + 1)
                if more(p):
                    split_y(p + 2)
                router(p)
                add_context(p + 1)
                finish(p)
                split_conv(p + 1)

            def last():
                router(NP - 1)
                finish(NP - 1)

            phases(dve, head, step, last)


ROUTE_EXP, ROUTE_ALL = 3, 12


def build(nc, d, out):
    y_dram = nc.dram_tensor("y_scratch", (NP, P, NG, P), F32).ap()
    with ExitStack() as ctx:
        with ExitStack() as front:
            bank = [front.enter_context(nc.psum_tensor(f"bank{i}", [P, 512], F32)) for i in range(8)]
            zhi = front.enter_context(nc.sbuf_tensor("z_hi", [P, KC, TOK], F32R))
            zlo = front.enter_context(nc.sbuf_tensor("z_lo", [P, KC, TOK], F32R))
            mix_phase(nc, d, bank, zhi, zlo, zhi[:, :, :].bitcast(F32))
            attention_phase(nc, d, bank, zhi, zlo, y_dram)
        bank2 = [ctx.enter_context(nc.psum_tensor(f"wide{i}", [P, 1024], F32)) for i in range(4)]
        ffn_phase(nc, d, bank2, y_dram, out)


def constants():
    theta = (1.0 / 10000.0 ** (np.arange(0, HD, 2, dtype=np.float32) / HD)).astype(np.float32)
    angle = np.outer(np.arange(NC, dtype=np.float32), theta).astype(np.float32)
    cos = np.cos(angle).astype(np.float32).T
    sin = np.sin(angle).astype(np.float32).T
    q, k = np.arange(P)[:, None] % NC, np.arange(NC)[None, :]
    return {
        "cos": np.tile(np.concatenate([cos, cos], 0), (GH, 1)),
        "sin": np.tile(np.concatenate([-sin, sin], 0), (GH, 1)),
        "mask": np.where(k <= q, 0.0, -1e30).astype(np.float32),
        "ident": np.eye(P, dtype=np.float32),
        "iota": np.tile(np.arange(NE, dtype=np.float32), (P, 1)),
    }


def layouts(v):
    w = v["L0_cond2_weight"]
    toep = np.zeros((P, 6, P), np.float32)
    for h in range(2):
        for j in range(3):
            for f in range(PH):
                for q in range(PH):
                    tap = PH * (j - 1) + f - q + TAPS // 2
                    if 0 <= tap < TAPS:
                        for gr in range(HC // CG):
                            o = h * HC + gr * CG
                            toep[f * HC + gr * CG:f * HC + (gr + 1) * CG, 3 * h + j,
                                 q * HC + gr * CG:q * HC + (gr + 1) * CG] = w[o:o + CG, :, tap].T
    last = np.concatenate([v["L0_ffn_W_base"], v["L0_ffn_A"].reshape(NE * RANK, L), v["L0_ffn_W_router"]], 0)
    mixw = np.concatenate([v["L0_cond_weight"][..., 0], v["L0_cond_bias_k"][:, :, None]], 2)
    return {
        "x": v["x"],
        "condT": v["cond_128"].T,
        "W0": v["L0_cond_W0"], "W1": v["L0_cond_W1"], "W2": v["L0_cond_W2"],
        "b0": v["L0_cond_b0"][:, None], "b1": v["L0_cond_b1"][:, None], "b2": v["L0_cond_b2"][None],
        "mixw": mixw,
        "wqkvT": v["L0_attn_w_attn"].reshape(3, NG, P, KC, P).transpose(1, 4, 3, 0, 2),
        "wteT": v["L0_attn_adapter_wte"].reshape(NA, KC, P).transpose(2, 1, 0),
        "gate": np.broadcast_to(v["L0_attn_gating"], (P, 1)),
        "wprojT": v["L0_attn_w_proj"].T.reshape(KC, P, L),
        "wffnT": last.T.reshape(2, P, PH, NF).transpose(0, 2, 1, 3).reshape(KC, P, NF),
        "loraB": v["L0_ffn_B"].transpose(0, 2, 1).reshape(NE * RANK, L),
        "toep": toep,
        "bbase": np.broadcast_to(v["L0_ffn_b_base"], (P, L)),
        "cwT": v["L0_cond2_c_weight"].T,
        "fside": np.broadcast_to(v["fside_S_0"], (P, NC)),
    }


def kernel(**inputs):
    import concourse.bacc as bacc
    from concourse.bass_utils import run_bass_kernel_spmd as run

    nc = bacc.Bacc("TRN2", target_bir_lowering=False, num_devices=1, dynamic_dma_scratch_size=DMA_RING)
    arrays, d = {}, {}
    for name, a in {**layouts({k: np.asarray(a) for k, a in inputs.items()}), **constants()}.items():
        a = np.ascontiguousarray(a)
        arrays[f"in_{name}"] = a
        d[name] = nc.dram_tensor(f"in_{name}", a.shape, mybir.dt.from_np(a.dtype), kind="ExternalInput").ap()
    out = nc.dram_tensor("out_0", (NB, NC, L), F32, kind="ExternalOutput").ap()
    build(nc, d, out)
    r = run(nc, [arrays], core_ids=[0])
    return r.results[0]["out_0"]
```

```python
from contextlib import ExitStack

import numpy as np

import concourse.bass as bass
from concourse import mybir

F32 = mybir.dt.float32
F32R = mybir.dt.float32r
U32 = mybir.dt.uint32
ALU = mybir.AluOpType
ACT = mybir.ActivationFunctionType
AX = mybir.AxisListType.X
ds = bass.ds

P = 128
NB, NC, L = 32, 64, 1024
TOK = NB * NC
HD = 32
GH = P // HD
NG = L // P
UT = 512
NU = TOK // UT
UB = UT // NC
UP = UB // 2
KC = L // P
NP = NB // 2
NA = 10
NE, RANK = 8, 16
NM = 8
OB = NC * NM // P
TAPS, CG = 9, 16
PH = 4
HC = 32
NF = L + NE * RANK + NE
SCALE = 1.0 / float(np.sqrt(HD))
ASCALE = 1.0 / float(np.sqrt(L))
LORA_SCALE = 32 / RANK
HALF_SWAP = [(i + HD // 2) % HD for i in range(HD)]
Q_, K_, V_ = 0, 1, 2
DMA_RING = 1024


def wait(eng, sem, value):
    if not isinstance(value, int) or value > 0:
        eng.wait_ge(sem, value)


def split_passes(hi_l, lo_l, hi_r, lo_r):
    return ((hi_l, hi_r), (hi_l, lo_r), (lo_l, hi_r))


def mix_phase(nc, d, bank, zhi, zlo, zhi_f, first_weights):
    wst, whi, wlo, whi_f, w_in, w_hi, w_lo = first_weights
    NX = 4
    DC = 3
    with ExitStack() as ctx:
        def sb(name, shape, dt=F32):
            return ctx.enter_context(nc.sbuf_tensor(name, shape, dt))

        def sem(name):
            return ctx.enter_context(nc.semaphore(name))

        condT = sb("m_condT", [P, NB])
        w0 = sb("m_w0", [P, P])
        w1 = sb("m_w1", [P, P])
        w2 = sb("m_w2", [P, NM])
        b0 = sb("m_b0", [P, 1])
        b1 = sb("m_b1", [P, 1])
        b2 = sb("m_b2", [1, NM])
        biask = sb("m_biask", [P, OB])
        biask_wide = sb("m_biask_wide", [P, OB, P])
        ones = sb("m_ones", [1, NB])
        ident = sb("m_ident", [NB, NB])
        mixw = sb("m_mixw", [P, OB, NC])
        pick = sb("m_pick", [P, P // NM])
        h0 = sb("m_h0", [P, NB])
        h1 = sb("m_h1", [P, NB])
        att = sb("m_att", [NB, NM])
        stat = sb("m_stat", [NB, 4])
        att_wide = sb("m_att_wide", [NB, P // NM, NM])
        att_sel = sb("m_att_sel", [P, 2, P // NM, NP])
        aggT = sb("m_aggT", [P, NP, 2, NC])
        aggb = sb("m_aggb", [P, TOK])
        xbuf = [sb(f"m_x{j}", [P, L]) for j in range(NX)]
        zt = [sb(f"m_z{j}", [P, KC, P]) for j in range(NX)]

        consts = sem("m_consts")
        ones_set = sem("m_ones_set")
        cleared = sem("m_cleared")
        mlp_mm = sem("m_mlp_mm")
        mlp_act = sem("m_mlp_act")
        soft = sem("m_soft")
        soft_exp = sem("m_soft_exp")
        bias_wide = sem("m_bias_wide")
        att_turned = sem("m_att_turned")
        att_spread = sem("m_att_spread")
        agg_mm = sem("m_agg_mm")
        agg_copied = sem("m_agg_copied")
        aggb_mm = sem("m_aggb_mm")
        aggb_copied = [sem(f"m_aggb_copied{k}") for k in range(2)]
        x_in = [sem(f"m_x_in{j}") for j in range(NX)]
        z_mm = [sem(f"m_z_mm{j}") for j in range(NX)]
        z_sum = [sem(f"m_z_sum{j}") for j in range(NX)]
        z_hi = [sem(f"m_z_hi{j}") for j in range(NX)]
        z_lo_dve = [sem(f"m_z_lo_dve{j}") for j in range(NX)]
        z_lo_pool = [sem(f"m_z_lo_pool{j}") for j in range(NX)]
        NCONST = 11
        agg_psum, aggb_psum = bank[4:6], (bank[6], bank[7])

        block = ctx.enter_context(nc.Block())

        def turns(eng, turn):
            turn(0)
            with eng.Fori(1, NP // NX) as it:
                turn(it)

        @block.sync
        def _(sp):
            for dst, src in ((condT, "condT"), (w0, "W0"), (b0, "b0"), (w1, "W1"), (b1, "b1"), (w2, "W2"),
                             (b2, "b2"), (biask, "biask")):
                sp.dma_start(dst[:], d[src]).then_inc(consts, 16)
            sp.dma_start(mixw[:], d["mixw"]).then_inc(consts, 16)
            sp.dma_start(pick[:], d["pick"]).then_inc(consts, 16)
            sp.dma_start(ident[:], d["ident"][0:NB, 0:NB]).then_inc(consts, 16)
            for j in range(2):
                sp.dma_start(xbuf[j][:], d["x"][2 * j:2 * j + 2].rearrange("b c l -> (b c) l")).then_inc(x_in[j], 16)
            sp.dma_start(wst[:], d["wqkvT"][0]).then_inc(w_in, 16)
            for j in range(2, NX):
                sp.dma_start(xbuf[j][:], d["x"][2 * j:2 * j + 2].rearrange("b c l -> (b c) l")).then_inc(x_in[j], 16)
            with sp.Fori(1, NP // NX) as it:
                for j in range(NX):
                    sp.wait_ge(z_mm[j], it)
                    sp.dma_start(xbuf[j][:], d["x"][ds((it * NX + j) * 2, 2)].rearrange("b c l -> (b c) l")
                                 ).then_inc(x_in[j], 16)

        @block.tensor
        def _(pe):
            pe.wait_ge(consts, 16 * NCONST)
            pe.wait_ge(ones_set, 1)
            pe.matmul(bank[0][:, 0:NB], w0[:], condT[:], start=True, stop=True).then_inc(mlp_mm, 1)
            pe.wait_ge(mlp_act, 1)
            pe.matmul(bank[0][:, 64:64 + NB], w1[:], h0[:], start=True, stop=True).then_inc(mlp_mm, 1)
            pe.wait_ge(mlp_act, 2)
            pe.matmul(bank[0][0:NB, 128:128 + NM], h1[:], w2[:], start=True, stop=False)
            pe.matmul(bank[0][0:NB, 128:128 + NM], ones[0:1, 0:NB], b2[:], start=False, stop=True).then_inc(mlp_mm, 1)
            pe.wait_ge(soft, 5)
            pe.matmul(bank[1][:, 0:NB], att_wide[:].rearrange("b o k -> b (o k)"), ident[:], start=True, stop=True
                      ).then_inc(att_turned, 1)
            pe.wait_ge(att_spread, 1)
            for n in range(OB):
                for b in range(2):
                    mm = pe.matmul(agg_psum[n // 2][NC * b:NC * (b + 1), 256 * (n % 2):256 * (n % 2 + 1)],
                                   mixw[:, n, :], att_sel[:, b, :, :].rearrange("p o i -> p (o i)"),
                                   start=True, stop=True)
                if n % 2:
                    mm.then_inc(agg_mm, 1)
            pe.wait_ge(bias_wide, 1)
            for n in range(OB):
                wait(pe, aggb_copied[n % 2], n // 2)
                pe.matmul(aggb_psum[n % 2][:], biask_wide[:, n, :], att_sel[:].rearrange("p b o i -> p (b o i)"),
                          start=True, stop=True).then_inc(aggb_mm, 1)
            pe.wait_ge(agg_copied, 4)
            for k in range(2):
                pe.wait_ge(aggb_copied[k], 2)

            def turn(it):
                for j in range(NX):
                    pe.wait_ge(x_in[j], 16 * it + 16)
                    wait(pe, z_sum[j], it)
                    for c in range(KC):
                        mm = pe.matmul(bank[2 * j + c // 4][:, (c % 4) * P:(c % 4 + 1) * P],
                                       xbuf[j][:, c * P:(c + 1) * P],
                                       aggT[:, ds(it * NX + j, 1), :, :].rearrange("p a b o -> p (a b o)"),
                                       start=True, stop=True)
                    mm.then_inc(z_mm[j], 1)

            turns(pe, turn)

        def agg_copy(copy, q, b):
            return copy(aggT[NC * b:NC * (b + 1), :, b, 32 * q:32 * q + 32].rearrange("p b o -> p o b"),
                        agg_psum[q][NC * b:NC * (b + 1), :].rearrange("p (o b) -> p o b", b=NP))

        def bias_copy(copy, n):
            o = P // NM
            return copy(aggb[:].rearrange("p (i b o) -> p b o i", b=2, o=NC)[:, :, n * o:(n + 1) * o, :],
                        aggb_psum[n % 2][:].rearrange("p (b o i) -> p b o i", b=2, i=NP))

        @block.scalar
        def _(act):
            for n, (h, b) in enumerate(((h0, b0), (h1, b1))):
                act.wait_ge(mlp_mm, n + 1)
                act.activation(h[:], bank[0][:, 64 * n:64 * n + NB], ACT.Gelu, bias=b[:, 0:1]).then_inc(mlp_act, 1)
            act.wait_ge(soft, 2)
            act.activation(att[:], att[:], ACT.Exp).then_inc(soft_exp, 1)
            act.wait_ge(agg_mm, 1)
            act.wait_ge(cleared, 1)
            for b in range(2):
                agg_copy(lambda o, i: act.activation(o, i, ACT.Copy), 0, b).then_inc(agg_copied, 1)
            for n in range(1, OB, 2):
                act.wait_ge(aggb_mm, n + 1)
                bias_copy(lambda o, i: act.activation(o, i, ACT.Copy), n).then_inc(aggb_copied[1], 1)
            for x in (K_, Q_, V_):
                act.wait_ge(w_in, 16)
                act.activation(whi[:, :, x, :], wst[:, :, x, :], ACT.Copy).then_inc(w_hi[x], 1)

            def turn(it):
                for j in range(NX):
                    act.wait_ge(z_sum[j], it + 1)
                    act.activation(zhi[:, :, ds((it * NX + j) * P, P)], zt[j][:], ACT.Copy).then_inc(z_hi[j], 1)

            turns(act, turn)

        def z_lo(eng, it, j, c0, c1):
            cols = ds((it * NX + j) * P, P)
            return eng.tensor_tensor(zlo[:, c0:c1, cols], zt[j][:, c0:c1, :], zhi_f[:, c0:c1, cols], ALU.subtract)

        @block.gpsimd
        def _(pool):
            pool.memset(aggT[:], 0.0).then_inc(cleared, 1)

            def turn(it):
                for j in range(NX):
                    pool.wait_ge(z_hi[j], it + 1)
                    z_lo(pool, it, j, DC, KC).then_inc(z_lo_pool[j], 1)

            turns(pool, turn)

        @block.vector
        def _(dve):
            dve.memset(ones[:], 1.0).then_inc(ones_set, 1)
            dve.wait_ge(consts, 16 * NCONST)
            dve.tensor_copy(biask_wide[:], biask[:].rearrange("p (n a) -> p n a", a=1).broadcast_to([P, OB, P])
                            ).then_inc(bias_wide, 1)
            dve.wait_ge(mlp_mm, 3)
            dve.reduce_max(stat[:, 0:1], bank[0][0:NB, 128:128 + NM], AX).then_inc(soft, 1)
            dve.wait_ge(soft, 1)
            dve.tensor_scalar(att[:], bank[0][0:NB, 128:128 + NM], stat[:, 0:1], None, ALU.subtract).then_inc(soft, 1)
            dve.wait_ge(soft_exp, 1)
            dve.reduce_sum(stat[:, 1:2], att[:], AX).then_inc(soft, 1)
            dve.wait_ge(soft, 3)
            dve.reciprocal(stat[:, 2:3], stat[:, 1:2]).then_inc(soft, 1)
            dve.wait_ge(soft, 4)
            dve.tensor_scalar(att_wide[:], att[:].rearrange("b (a k) -> b a k", a=1).broadcast_to([NB, P // NM, NM]),
                              stat[:, 2:3], None, ALU.mult).then_inc(soft, 1)
            dve.wait_ge(att_turned, 1)
            dve.tensor_tensor(
                att_sel[:],
                bank[1][:, 0:NB].rearrange("p (i b a) -> p b a i", b=2, a=1).broadcast_to([P, 2, P // NM, NP]),
                pick[:].rearrange("p (b o a) -> p b o a", b=1, a=1).broadcast_to([P, 2, P // NM, NP]), ALU.mult
                ).then_inc(att_spread, 1)
            dve.wait_ge(agg_mm, 2)
            dve.wait_ge(cleared, 1)
            for b in range(2):
                agg_copy(dve.tensor_copy, 1, b).then_inc(agg_copied, 1)
            for n in range(0, OB, 2):
                dve.wait_ge(aggb_mm, n + 1)
                bias_copy(dve.tensor_copy, n).then_inc(aggb_copied[0], 1)
            for k in range(2):
                dve.wait_ge(aggb_copied[k], 2)
            for x in (K_, Q_, V_):
                dve.wait_ge(w_hi[x], 1)
                dve.tensor_tensor(wlo[:, :, x, :], wst[:, :, x, :], whi_f[:, :, x, :], ALU.subtract
                                  ).then_inc(w_lo[x], 1)

            def turn(it):
                for j in range(NX):
                    dve.wait_ge(z_mm[j], it + 1)
                    wait(dve, z_lo_pool[j], it)
                    wait(dve, z_lo_dve[j], it)
                    for half in range(2):
                        z = dve.tensor_tensor(
                            zt[j][:, 4 * half:4 * half + 4, :],
                            bank[2 * j + half][:].rearrange("p (c t) -> p c t", t=P),
                            aggb[:, ds((it * NX + j) * P, P)].rearrange("p (a t) -> p a t", a=1).broadcast_to([P, 4, P]),
                            ALU.add)
                    z.then_inc(z_sum[j], 1)
                    if j >= 1:
                        dve.wait_ge(z_hi[j - 1], it + 1)
                        z_lo(dve, it, j - 1, 0, DC).then_inc(z_lo_dve[j - 1], 1)
                dve.wait_ge(z_hi[NX - 1], it + 1)
                z_lo(dve, it, NX - 1, 0, DC).then_inc(z_lo_dve[NX - 1], 1)

            turns(dve, turn)


def attention_phase(nc, d, bank, zhi, zlo, y_dram, weights):
    wst, whi, wlo, whi_f, w_in, w_hi, w_lo = weights
    with ExitStack() as ctx:
        def sb(name, shape, dt=F32):
            return ctx.enter_context(nc.sbuf_tensor(name, shape, dt))

        def sem(name):
            return ctx.enter_context(nc.semaphore(name))

        wte = sb("a_wte", [P, KC, NA])
        wtehi = sb("a_wtehi", [P, KC, P], F32R)
        wtelo = sb("a_wtelo", [P, KC, P], F32R)
        wtehi_f = wtehi[:, :, :].bitcast(F32)
        cosT = sb("a_cos", [P, NC])
        sinT = sb("a_sin", [P, NC])
        mask = sb("a_mask", [P, NC])
        ident = sb("a_ident", [P, P])
        gate = sb("a_gate", [P, 1])
        qr = sb("a_qr", [P, UT])
        kr = sb("a_kr", [P, UT])
        rot = sb("a_rot", [P, UT])
        kbd = sb("a_kbd", [P, UB, GH, NC])
        vT = sb("a_vT", [P, UT])
        vbd = sb("a_vbd", [P, UP, 2, 2, 2 * HD])
        prob = [sb(f"a_prob{t}", [P, 8, NC]) for t in range(2)]
        pT = [sb(f"a_pT{t}", [P, 2, 2, P]) for t in range(2)]
        stat = sb("a_stat", [P, 2, 3, 8])
        aprob = sb("a_aprob", [P, UP, GH, HD])
        atmp = sb("a_atmp", [P, UP * GH, NA])
        astat = sb("a_astat", [P, 3, UP * GH])
        aT = sb("a_aT", [P, UT])
        akv = sb("a_akv", [NA, 2 * P])
        akbd = sb("a_akbd", [P, GH, NA])
        avbd = sb("a_avbd", [P, P])
        ysb = sb("a_ysb", [P, UT])

        bS, bPT, bY, bAD, bQ, bK, bV = bank[0:2], bank[2], bank[3], bank[4], bank[5], bank[6], bank[7]
        AKT = 2 * P

        consts = sem("a_consts")
        cleared = sem("a_cleared")
        wte_hi = sem("a_wte_hi")
        wte_lo = sem("a_wte_lo")
        mm_done = {Q_: sem("a_q_mm"), K_: sem("a_k_mm"), V_: sem("a_v_mm")}
        turned = {Q_: sem("a_q_turned"), K_: sem("a_k_turned")}
        rotated = {Q_: sem("a_q_rotated"), K_: sem("a_k_rotated")}
        rot_step = sem("a_rot_step")
        kbd_set = sem("a_kbd_set")
        vT_copied = sem("a_vT_copied")
        v_tr = sem("a_v_tr")
        vbd_set = sem("a_vbd_set")
        scores = sem("a_scores")
        masked = sem("a_masked")
        row_max = sem("a_row_max")
        shifted = sem("a_shifted")
        exped = sem("a_exped")
        row_sum = sem("a_row_sum")
        inverted = sem("a_inverted")
        probs = sem("a_probs")
        p_tr = sem("a_p_tr")
        pT_copied = sem("a_pT_copied")
        ascores = sem("a_ascores")
        amax = sem("a_amax")
        ashifted = sem("a_ashifted")
        aexped = sem("a_aexped")
        asum = sem("a_asum")
        ainv = sem("a_ainv")
        agated = sem("a_agated")
        aprobs = sem("a_aprobs")
        a_tr = sem("a_a_tr")
        aT_copied = sem("a_aT_copied")
        akv_mm = sem("a_akv_mm")
        akv_copied = sem("a_akv_copied")
        ak_tr = sem("a_ak_tr")
        akbd_set = sem("a_akbd_set")
        avbd_set = sem("a_avbd_set")
        y_mm = sem("a_y_mm")
        y_copied = sem("a_y_copied")
        y_out = sem("a_y_out")
        NCONST, NCLEAR = 6, 7

        block = ctx.enter_context(nc.Block())

        def phases(eng, step, tail):
            for u in range(NU // 2):
                step(0, u)
            with eng.Fori(0, NG - 1) as g:
                for u in range(NU // 2, NU):
                    step(g, u)
                for u in range(NU // 2):
                    step(g + 1, u)
            for u in range(NU // 2, NU):
                step(NG - 1, u)
            tail()

        def first(g, u):
            return isinstance(g, int) and g == 0 and u == 0

        def refill(g, u):
            return u == NU - 1 and not (isinstance(g, int) and g == NG - 1)

        @block.sync
        def _(sp):
            for dst, src in ((wte, "wteT"), (cosT, "cos"), (sinT, "sin"), (mask, "mask"), (ident, "ident"),
                             (gate, "gate")):
                sp.dma_start(dst[:], d[src]).then_inc(consts, 16)

            def store(g, u):
                sp.wait_ge(y_copied, NU * g + u + 1)
                sp.dma_start(y_dram[u * UP:(u + 1) * UP, :, ds(g, 1), :].rearrange("i p a t -> p i (a t)"),
                             ysb[:].rearrange("p (i t) -> p i t", i=UP)).then_inc(y_out, 16)

            def step(g, u):
                if not first(g, u):
                    store(*((g, u - 1) if u else (g - 1, NU - 1)))
                if u == 2 and not (isinstance(g, int) and g == NG - 1):
                    for x in (Q_, K_, V_):
                        sp.wait_ge(w_lo[x], g + 1)
                    sp.dma_start(wst[:], d["wqkvT"][ds(g + 1, 1)].rearrange("a p k x c -> p (a k) x c")
                                 ).then_inc(w_in, 16)

            def tail():
                store(NG - 1, NU - 1)
                sp.wait_ge(y_out, 16 * NG * NU)

            phases(sp, step, tail)

        @block.gpsimd
        def _(pool):
            for t in (kbd, vbd, aprob, avbd, akbd):
                pool.memset(t[:], 0.0).then_inc(cleared, 1)
            for t in (wtehi, wtelo):
                pool.memset(t[:].bitcast(F32), 0.0).then_inc(cleared, 1)

        @block.tensor
        def _(pe):
            def attend_scores(m):
                pe.wait_ge(rotated[Q_], m + 1)
                pe.wait_ge(kbd_set, m + 1)
                wait(pe, aT_copied, m)
                wait(pe, pT_copied, 2 * m)
                for s in range(UP):
                    for b in range(2):
                        mm = pe.matmul(bS[s // 2][NC * b:NC * b + NC, (s % 2) * GH * NC:(s % 2 + 1) * GH * NC],
                                       qr[:, (2 * s + b) * NC:(2 * s + b + 1) * NC],
                                       kbd[:, 2 * s + b, :, :].rearrange("p h k -> p (h k)"), start=True, stop=True)
                    if s % 2:
                        mm.then_inc(scores, 1)

            def attend_ascores(m, groups):
                wait(pe, ashifted, m)
                pe.wait_ge(akbd_set, groups)
                for i in range(UP):
                    for b in range(2):
                        mm = pe.matmul(bAD[NC * b:NC * (b + 1), i * GH * NA:(i + 1) * GH * NA],
                                       qr[:, (2 * i + b) * NC:(2 * i + b + 1) * NC],
                                       akbd[:].rearrange("p h a -> p (h a)"), start=True, stop=True)
                mm.then_inc(ascores, 1)

            def attend_transposes(m):
                pe.wait_ge(aprobs, m + 1)
                for i in range(UP):
                    tr = pe.transpose(bS[0][:, i * P:(i + 1) * P], aprob[:, i, :, :].rearrange("p h a -> p (h a)"),
                                      ident[:])
                tr.then_inc(a_tr, 1)
                wait(pe, pT_copied, 2 * m)
                for t, dst in ((0, bPT), (1, bS[1])):
                    pe.wait_ge(probs, 2 * m + t + 1)
                    for j in range(4):
                        tr = pe.transpose(dst[:, j * P:(j + 1) * P],
                                          prob[t][:, 2 * j:2 * j + 2, :].rearrange("p h k -> p (h k)"), ident[:])
                    tr.then_inc(p_tr, 1)

            def attend_values(m, groups):
                pe.wait_ge(aT_copied, m + 1)
                pe.wait_ge(avbd_set, groups)
                wait(pe, y_copied, m)
                pe.matmul(bY[:], avbd[:], aT[:], start=True, stop=True)
                pe.wait_ge(vbd_set, m + 1)
                for s in range(UP):
                    if s % 2 == 0:
                        pe.wait_ge(pT_copied, 2 * m + s // 2 + 1)
                    for b in range(2):
                        for hp in range(2):
                            mm = pe.matmul(bY[2 * HD * hp:2 * HD * (hp + 1), (2 * s + b) * NC:(2 * s + b + 1) * NC],
                                           vbd[:, s, b, hp, :], pT[s // 2][:, s % 2, hp, NC * b:NC * b + NC],
                                           start=False, stop=True, skip_group_check=True)
                mm.then_inc(y_mm, 1)

            def project(x, dst, g, u):
                pe.wait_ge(w_lo[x], g + 1)
                for c in range(KC):
                    for i, (w, z) in enumerate(split_passes(whi, wlo, zhi, zlo)):
                        mm = pe.matmul(dst[:], w[:, c, x, :], z[:, c, u * UT:(u + 1) * UT],
                                       start=(c == 0 and i == 0), stop=(c == KC - 1 and i == 2))
                mm.then_inc(mm_done[x], 1)

            def step(g, u):
                n = NU * g + u
                groups = g + 1 if u else g
                att = not first(g, u)
                if att:
                    attend_scores(n - 1)
                    attend_ascores(n - 1, groups)
                wait(pe, turned[K_], n)
                project(K_, bK, g, u)
                wait(pe, turned[Q_], n)
                project(Q_, bQ, g, u)
                if att:
                    attend_transposes(n - 1)
                wait(pe, vbd_set, n)
                project(V_, bV, g, u)
                if u == 0:
                    pe.wait_ge(wte_lo, 1)
                    wait(pe, ashifted, n)
                    for c in range(KC):
                        for i, (a, w) in enumerate(split_passes(wtehi, wtelo, whi, wlo)):
                            mm = pe.matmul(bAD[:, 0:2 * P], a[:, c, :], w[:, c, K_:V_ + 1, :].rearrange("p x c -> p (x c)"),
                                           start=(c == 0 and i == 0), stop=(c == KC - 1 and i == 2))
                    mm.then_inc(akv_mm, 1)
                if att:
                    attend_values(n - 1, groups)
                if u == 0:
                    pe.wait_ge(akv_copied, g + 1)
                pe.wait_ge(vT_copied, n + 1)
                for i in range(UP):
                    tr = pe.transpose(bV[:, i * P:(i + 1) * P], vT[:, i * P:(i + 1) * P], ident[:])
                tr.then_inc(v_tr, 1)
                if u == 0:
                    pe.transpose(bAD[:, AKT:AKT + NA], akv[:, 0:P], ident[0:NA, 0:NA]).then_inc(ak_tr, 1)

            def tail():
                m = NG * NU - 1
                attend_scores(m)
                attend_ascores(m, NG)
                attend_transposes(m)
                attend_values(m, NG)

            phases(pe, step, tail)

        @block.scalar
        def _(act):
            act.wait_ge(consts, 16 * NCONST)
            act.wait_ge(cleared, NCLEAR)
            act.activation(wtehi[:, :, 0:NA], wte[:], ACT.Copy).then_inc(wte_hi, 1)

            def split_hi(x, g, n):
                act.wait_ge(w_in, 16 * g + 16)
                wait(act, mm_done[x], n)
                if x != Q_:
                    wait(act, akv_mm, g)
                act.activation(whi[:, :, x, :], wst[:, :, x, :], ACT.Copy).then_inc(w_hi[x], 1)

            def attend_exp(m):
                for t in range(2):
                    act.wait_ge(shifted, 2 * m + t + 1)
                    act.activation(prob[t][:], prob[t][:], ACT.Exp, scale=SCALE).then_inc(exped, 1)
                act.wait_ge(ashifted, m + 1)
                act.activation(atmp[:], atmp[:], ACT.Exp, scale=ASCALE).then_inc(aexped, 1)

            def attend_copies(m):
                act.wait_ge(a_tr, m + 1)
                wait(act, y_mm, m)
                act.activation(aT[:], bS[0][:], ACT.Copy).then_inc(aT_copied, 1)
                for t, src in ((0, bPT), (1, bS[1])):
                    act.wait_ge(p_tr, 2 * m + t + 1)
                    act.activation(pT[t][:].rearrange("p s h q -> p (s h q)"), src[:], ACT.Copy).then_inc(pT_copied, 1)

            def y_copy(m):
                act.wait_ge(y_mm, m + 1)
                wait(act, y_out, 16 * m)
                act.activation(ysb[:], bY[:], ACT.Copy).then_inc(y_copied, 1)

            def step(g, u):
                n = NU * g + u
                att = not first(g, u)
                if att:
                    attend_exp(n - 1)
                act.wait_ge(rotated[K_], n + 1)
                wait(act, scores, 2 * n)
                for h in range(GH):
                    cp = act.activation(kbd[HD * h:HD * (h + 1), :, h, :],
                                        kr[HD * h:HD * (h + 1), :].rearrange("p (b k) -> p b k", k=NC), ACT.Copy)
                cp.then_inc(kbd_set, 1)
                if refill(g, u):
                    split_hi(K_, g + 1, n + 1)
                if att:
                    attend_copies(n - 1)
                if refill(g, u):
                    split_hi(Q_, g + 1, n + 1)
                act.wait_ge(mm_done[V_], n + 1)
                wait(act, v_tr, n)
                act.activation(vT[:], bV[:], ACT.Copy).then_inc(vT_copied, 1)
                if refill(g, u):
                    split_hi(V_, g + 1, n + 1)
                if u == 0:
                    act.wait_ge(akv_mm, g + 1)
                    wait(act, avbd_set, g)
                    wait(act, ak_tr, g)
                    act.activation(akv[:], bAD[0:NA, 0:2 * P], ACT.Copy).then_inc(akv_copied, 1)
                if att:
                    y_copy(n - 1)
                if u == 0:
                    act.wait_ge(akv_copied, g + 1)
                    wait(act, y_mm, n)
                    for h in range(GH):
                        cp = act.activation(avbd[HD * h:HD * h + NA, HD * h:HD * (h + 1)],
                                            akv[:, P + HD * h:P + HD * (h + 1)], ACT.Copy)
                    cp.then_inc(avbd_set, 1)
                    act.wait_ge(ak_tr, g + 1)
                    wait(act, ascores, n)
                    for h in range(GH):
                        cp = act.activation(akbd[HD * h:HD * (h + 1), h, :], bAD[HD * h:HD * (h + 1), AKT:AKT + NA],
                                            ACT.Copy)
                    cp.then_inc(akbd_set, 1)
                act.wait_ge(v_tr, n + 1)
                wait(act, y_mm, n)
                for b in range(2):
                    for h in range(2):
                        cp = act.activation(
                            vbd[NC * h:NC * (h + 1), :, b, :, HD * h:HD * (h + 1)],
                            bV[NC * b:NC * (b + 1), :].rearrange("p (s a h e) -> p s a h e", s=UP, a=2, h=2)[:, :, :, h, :],
                            ACT.Copy)
                cp.then_inc(vbd_set, 1)

            def tail():
                m = NG * NU - 1
                attend_exp(m)
                attend_copies(m)
                y_copy(m)

            phases(act, step, tail)

        @block.vector
        def _(dve):
            dve.wait_ge(wte_hi, 1)
            dve.tensor_tensor(wtelo[:, :, 0:NA], wte[:], wtehi_f[:, :, 0:NA], ALU.subtract).then_inc(wte_lo, 1)

            def split_lo(x, g, n):
                dve.wait_ge(w_hi[x], g + 1)
                wait(dve, mm_done[x], n)
                if x != Q_:
                    wait(dve, akv_mm, g)
                dve.tensor_tensor(wlo[:, :, x, :], wst[:, :, x, :], whi_f[:, :, x, :], ALU.subtract
                                  ).then_inc(w_lo[x], 1)

            def rotate(x, src, dst, n, used, count):
                tab = [t[:].rearrange("p (a k) -> p a k", a=1).broadcast_to([P, UB, NC]) for t in (cosT, sinT)]
                i = 0 if x == K_ else 2
                dve.wait_ge(mm_done[x], n + 1)
                wait(dve, rotated[Q_ if x == K_ else K_], n if x == K_ else n + 1)
                for s, c in used:
                    wait(dve, s, c)
                dve.tensor_tensor(dst[:].rearrange("p (b k) -> p b k", k=NC),
                                  src[:].rearrange("p (b k) -> p b k", k=NC), tab[0], ALU.mult).then_inc(rot_step, 1)
                dve.stream_shuffle(rot[:], src[:], HALF_SWAP).then_inc(turned[x], 1)
                dve.wait_ge(turned[x], n + 1)
                r = rot[:].rearrange("p (b k) -> p b k", k=NC)
                dve.tensor_tensor(r, r, tab[1], ALU.mult).then_inc(rot_step, 1)
                dve.wait_ge(rot_step, 4 * n + i + 2)
                dve.tensor_tensor(dst[:], dst[:], rot[:], ALU.add).then_inc(rotated[x], 1)

            def attend_softmax(m):
                maskb = mask[:].rearrange("p (a k) -> p a k", a=1).broadcast_to([P, 8, NC])

                def spread(t, k):
                    return stat[:, t, k, :].rearrange("p (a b) -> p a b", b=1).broadcast_to([P, 8, NC])

                def aspread(k):
                    return astat[:, k, :].rearrange("p (a b) -> p a b", b=1).broadcast_to([P, UP * GH, NA])

                for t in range(2):
                    dve.wait_ge(scores, 2 * m + t + 1)
                    wait(dve, p_tr, 2 * m)
                    dve.tensor_tensor(prob[t][:], bS[t][:].rearrange("p (a k) -> p a k", k=NC), maskb, ALU.add
                                      ).then_inc(masked, 1)
                    dve.wait_ge(masked, 2 * m + t + 1)
                    dve.tensor_reduce(stat[:, t, 0, :], prob[t][:], AX, ALU.max).then_inc(row_max, 1)
                    dve.wait_ge(row_max, 2 * m + t + 1)
                    dve.tensor_tensor(prob[t][:], prob[t][:], spread(t, 0), ALU.subtract).then_inc(shifted, 1)
                dve.wait_ge(ascores, m + 1)
                asrc = bAD[:, 0:UP * GH * NA].rearrange("p (a k) -> p a k", k=NA)
                dve.tensor_reduce(astat[:, 0, :], asrc, AX, ALU.max).then_inc(amax, 1)
                dve.wait_ge(amax, m + 1)
                wait(dve, aprobs, m)
                dve.tensor_tensor(atmp[:], asrc, aspread(0), ALU.subtract).then_inc(ashifted, 1)
                for t in range(2):
                    dve.wait_ge(exped, 2 * m + t + 1)
                    dve.tensor_reduce(stat[:, t, 1, :], prob[t][:], AX, ALU.add).then_inc(row_sum, 1)
                    dve.wait_ge(row_sum, 2 * m + t + 1)
                    dve.reciprocal(stat[:, t, 2, :], stat[:, t, 1, :]).then_inc(inverted, 1)
                    dve.wait_ge(inverted, 2 * m + t + 1)
                    dve.tensor_tensor(prob[t][:], prob[t][:], spread(t, 2), ALU.mult).then_inc(probs, 1)
                dve.wait_ge(aexped, m + 1)
                dve.tensor_reduce(astat[:, 1, :], atmp[:], AX, ALU.add).then_inc(asum, 1)
                dve.wait_ge(asum, m + 1)
                dve.reciprocal(astat[:, 2, :], astat[:, 1, :]).then_inc(ainv, 1)
                dve.wait_ge(ainv, m + 1)
                dve.tensor_scalar(astat[:, 2, :], astat[:, 2, :], gate[:, 0:1], None, ALU.mult).then_inc(agated, 1)
                dve.wait_ge(agated, m + 1)
                wait(dve, a_tr, m)
                dve.tensor_tensor(aprob[:].rearrange("p i h a -> p (i h) a")[:, :, 0:NA], atmp[:], aspread(2), ALU.mult
                                  ).then_inc(aprobs, 1)

            def step(g, u):
                n = NU * g + u
                if not first(g, u):
                    attend_softmax(n - 1)
                rotate(K_, bK, kr, n, ((kbd_set, n),), n)
                if refill(g, u):
                    split_lo(K_, g + 1, n + 1)
                rotate(Q_, bQ, qr, n, ((scores, 2 * n), (ascores, n)), n)
                if refill(g, u):
                    split_lo(Q_, g + 1, n + 1)
                    split_lo(V_, g + 1, n + 1)

            phases(dve, step, lambda: attend_softmax(NG * NU - 1))


def ffn_phase(nc, d, bank2, y_dram, out):
    with ExitStack() as ctx:
        def sb(name, shape, dt=F32):
            return ctx.enter_context(nc.sbuf_tensor(name, shape, dt))

        def sem(name):
            return ctx.enter_context(nc.semaphore(name))

        bP, bF, bC, bT = bank2
        CW = 388
        cuts = [(512 * i, CW * i, min(CW * (i + 1), NF)) for i in range(3)]
        HID = 512 * 2 + L - 2 * CW

        wphi = sb("f_wphi", [P, KC, L], F32R)
        wplo = sb("f_wplo", [P, KC, L], F32R)
        wfhi = sb("f_wfhi", [P, KC, NF], F32R)
        wflo = sb("f_wflo", [P, KC, NF], F32R)
        NST = 3
        loraB = sb("f_loraB", [P, L])
        toep = sb("f_toep", [P, 6, P])
        ctxb = sb("f_ctxb", [P, TOK])
        bbase = sb("f_bbase", [P, L])
        ident = sb("f_ident", [P, P])
        iota = sb("f_iota", [P, NE])
        condT = sb("f_condT", [P, NB])
        cwT = sb("f_cwT", [P, NC])
        fside = sb("f_fside", [P, NC])
        ones = sb("f_ones", [P, P])
        yst = sb("f_yst", [P, KC, P])
        yhi = sb("f_yhi", [P, KC, P], F32R)
        ylo = sb("f_ylo", [P, KC, P], F32R)
        xt = sb("f_xt", [P, L])
        x1 = sb("f_x1", [P, L])
        x1b = sb("f_x1b", [P, L])
        XW = PH + L + PH
        x4 = sb("f_x4", [P, 2, 2, XW])
        wst = [x4[:].rearrange("p b h t -> p (b h t)")[:, i * NF:(i + 1) * NF] for i in range(NST)]
        ct = sb("f_ct", [P, KC, P])
        chi = sb("f_chi", [P, KC, P], F32R)
        clo = sb("f_clo", [P, KC, P], F32R)
        osb = sb("f_osb", [P, L])
        lg = sb("f_lg", [P, NE])
        top = sb("f_top", [P, 8])
        topi = sb("f_topi", [P, 8], U32)
        rs = sb("f_rs", [P, 8])
        we = sb("f_we", [P, 3, NE])
        hw = sb("f_hw", [P, P])
        hwT = sb("f_hwT", [P, P])

        consts = sem("f_consts")
        cleared = sem("f_cleared")
        w_in = [sem(f"f_w_in{i}") for i in range(NST)]
        w_hi = sem("f_w_hi")
        w_lo = sem("f_w_lo")
        prods = sem("f_prods")
        ctx_mm = sem("f_ctx_mm")
        ctx_set = sem("f_ctx_set")
        y_in = sem("f_y_in")
        y_hi = sem("f_y_hi")
        y_lo = sem("f_y_lo")
        x_in = sem("f_x_in")
        proj_mm = sem("f_proj_mm")
        x1_set = sem("f_x1_set")
        x1b_set = sem("f_x1b_set")
        x4_in = sem("f_x4_in")
        conv_mm = sem("f_conv_mm")
        conv_set = sem("f_conv_set")
        c_hi = sem("f_c_hi")
        c_lo = sem("f_c_lo")
        ffn_mm = sem("f_ffn_mm")
        route = sem("f_route")
        route_exp = sem("f_route_exp")
        hw_set = sem("f_hw_set")
        hw_tr = sem("f_hw_tr")
        hwT_set = sem("f_hwT_set")
        lora_mm = sem("f_lora_mm")
        out_set = sem("f_out_set")
        stored = sem("f_stored")
        NCONST = 8
        NX4 = 16
        weights = [("wprojT", c, wphi, wplo, L) for c in range(KC)] + [("wffnT", c, wfhi, wflo, NF) for c in range(KC)]
        NW = len(weights)

        block = ctx.enter_context(nc.Block())

        def phases(eng, head, step):
            head()
            step(0, 3)
            with eng.Fori(1, NP - 3) as p:
                step(p, 3)
            for p in range(NP - 3, NP):
                step(p, NP - 1 - p)

        @block.sync
        def _(sp):
            def load_w(i):
                name, c, _, _, n = weights[i]
                wait(sp, w_lo, i - NST + 1)
                sp.dma_start(wst[i % NST][:, 0:n], d[name][c]).then_inc(w_in[i % NST], 16)

            def load_y(p):
                wait(sp, y_lo, p)
                sp.dma_start(yst[:], y_dram[ds(p, 1)].rearrange("a p k t -> p (a k) t")).then_inc(y_in, 16)

            def load_x(p):
                wait(sp, x1_set, p)
                sp.dma_start(xt[:], d["x"][ds(p * 2, 2)].rearrange("b c l -> (b c) l")).then_inc(x_in, 16)

            def spread(p):
                sp.wait_ge(x1_set, p + 1)
                wait(sp, conv_mm, 2 * p)
                if isinstance(p, int) and p == 0:
                    sp.wait_ge(w_lo, NW)
                for b in range(2):
                    for h in range(2):
                        for f in range(PH):
                            r = b * NC + h * HC
                            sp.dma_start(x4[HC * f:HC * (f + 1), b, h, PH - f:PH - f + L], x1[r:r + HC, :]
                                         ).then_inc(x4_in, 16)

            def store(p):
                sp.wait_ge(out_set, p + 1)
                sp.dma_start(out[ds(p * 2, 2)].rearrange("b c l -> (b c) l"), osb[:]).then_inc(stored, 16)

            for i in range(NST):
                load_w(i)
            load_y(0)
            load_x(0)
            for dst, src in ((loraB, "loraB"), (toep, "toep"), (bbase, "bbase"), (ident, "ident"), (iota, "iota"),
                             (condT, "condT"), (cwT, "cwT"), (fside, "fside")):
                sp.dma_start(dst[:], d[src]).then_inc(consts, 16)
            for i in range(NST, NW):
                load_w(i)

            def head():
                load_y(1)
                spread(0)
                load_x(1)
                load_y(2)
                spread(1)

            def step(p, ahead):
                if ahead >= 2:
                    load_x(p + 2)
                if ahead >= 3:
                    load_y(p + 3)
                store(p)
                if ahead >= 2:
                    spread(p + 2)

            phases(sp, head, step)
            sp.wait_ge(stored, 16 * NP)

        @block.gpsimd
        def _(pool):
            pool.memset(ones[:], 1.0).then_inc(cleared, 1)
            pool.wait_ge(w_lo, NW)
            pool.memset(x4[:, :, :, 0:1], 0.0).then_inc(cleared, 1)
            pool.memset(x4[:, :, :, PH + L:PH + L + 1], 0.0).then_inc(cleared, 1)
            pool.wait_ge(consts, 16 * NCONST)

            def add_bias(p):
                pool.wait_ge(x1_set, p + 1)
                wait(pool, out_set, p)
                pool.tensor_tensor(x1b[:], x1[:], bbase[:], ALU.add).then_inc(x1b_set, 1)

            def step(p, ahead):
                if ahead >= 1:
                    add_bias(p + 1)

            phases(pool, lambda: add_bias(0), step)

        @block.tensor
        def _(pe):
            pe.wait_ge(cleared, 1)
            pe.wait_ge(consts, 16 * NCONST)
            for i in range(TOK // 512):
                pe.wait_ge(prods, i + 1)
                wait(pe, ctx_set, i - 1)
                pe.matmul(bC[:, (i % 2) * 512:(i % 2 + 1) * 512], ones[:], osb[:, (i % 2) * 512:(i % 2 + 1) * 512],
                          start=True, stop=True).then_inc(ctx_mm, 1)

            def project(p, c0, c1, head=False):
                if c0 == 0:
                    pe.wait_ge(y_lo, p + 1)
                    wait(pe, x1_set, p)
                for c in range(c0, c1):
                    if head:
                        pe.wait_ge(w_lo, c + 1)
                    for i, (y, w) in enumerate(split_passes(yhi, ylo, wphi, wplo)):
                        for n in range(2):
                            mm = pe.matmul(bP[:, n * 512:(n + 1) * 512], y[:, c, :], w[:, c, n * 512:(n + 1) * 512],
                                           start=(c == 0 and i == 0), stop=(c == KC - 1 and i == 2))
                if c1 == KC:
                    mm.then_inc(proj_mm, 1)

            def convolve(p):
                pe.wait_ge(x4_in, 16 * NX4 * (p + 1))
                wait(pe, conv_set, 2 * p)
                for k in range(2):
                    for b in range(2):
                        for h in range(2):
                            for j in range(3):
                                t = PH * (P * k + j)
                                o = (2 * k + b) * 256 + h * P
                                mm = pe.matmul(bC[:, o:o + P], x4[:, b, h, t:t + PH * (P - 1) + 1:PH],
                                               toep[:, 3 * h + j, :], start=(j == 0), stop=(j == 2))
                    mm.then_inc(conv_mm, 1)

            def last_layer(p):
                pe.wait_ge(c_lo, p + 1)
                wait(pe, out_set, p)
                for c in range(KC):
                    for i, (a, w) in enumerate(split_passes(chi, clo, wfhi, wflo)):
                        for at, n0, n1 in cuts:
                            mm = pe.matmul(bF[:, at:at + n1 - n0], a[:, c, :], w[:, c, n0:n1],
                                           start=(c == 0 and i == 0), stop=(c == KC - 1 and i == 2))
                mm.then_inc(ffn_mm, 1)

            def turn_hidden(p):
                pe.wait_ge(hw_set, p + 1)
                wait(pe, hwT_set, p)
                pe.transpose(bT[:, 0:P], hw[:], ident[:]).then_inc(hw_tr, 1)

            def low_rank(p):
                pe.wait_ge(hwT_set, p + 1)
                for at, n0, n1 in cuts:
                    n1 = min(n1, L)
                    mm = pe.matmul(bF[:, at:at + n1 - n0], hwT[:], loraB[:, n0:n1],
                                   start=False, stop=True, skip_group_check=True)
                mm.then_inc(lora_mm, 1)

            def head():
                project(0, 0, KC, head=True)
                project(1, 0, KC)
                pe.wait_ge(cleared, 3)
                convolve(0)
                pe.wait_ge(w_lo, NW)

            def step(p, ahead):
                last_layer(p)
                if ahead >= 2:
                    project(p + 2, 0, 3)
                turn_hidden(p)
                if ahead >= 2:
                    project(p + 2, 3, 5)
                low_rank(p)
                if ahead >= 1:
                    convolve(p + 1)
                if ahead >= 2:
                    project(p + 2, 5, KC)

            phases(pe, head, step)

        @block.scalar
        def _(act):
            def split_y(p):
                act.wait_ge(y_in, 16 * (p + 1))
                wait(act, proj_mm, p)
                act.activation(yhi[:], yst[:], ACT.Copy).then_inc(y_hi, 1)

            def split_conv(p):
                act.wait_ge(conv_set, 2 * (p + 1))
                wait(act, ffn_mm, p)
                act.activation(chi[:], ct[:], ACT.Copy).then_inc(c_hi, 1)

            def route_and_copy(p):
                act.wait_ge(route, ROUTE_EXP + ROUTE_ALL * p)
                act.activation(rs[:, 1:2], rs[:, 0:1], ACT.Exp).then_inc(route_exp, 1)
                act.wait_ge(hw_tr, p + 1)
                wait(act, lora_mm, p)
                act.activation(hwT[:], bT[:, 0:P], ACT.Copy).then_inc(hwT_set, 1)

            for i, (_, c, hi, _, n) in enumerate(weights):
                act.wait_ge(w_in[i % NST], 16 * (i // NST + 1))
                act.activation(hi[:, c, :], wst[i % NST][:, 0:n], ACT.Copy).then_inc(w_hi, 1)
                if i == 0:
                    split_y(0)

            def head():
                split_y(1)
                split_conv(0)

            def step(p, ahead):
                if ahead >= 2:
                    split_y(p + 2)
                route_and_copy(p)
                if ahead >= 1:
                    split_conv(p + 1)

            phases(act, head, step)

        @block.vector
        def _(dve):
            def split_y(p):
                dve.wait_ge(y_hi, p + 1)
                wait(dve, proj_mm, p)
                dve.tensor_tensor(ylo[:], yst[:], yhi[:].bitcast(F32), ALU.subtract).then_inc(y_lo, 1)

            def residual(p):
                dve.wait_ge(proj_mm, p + 1)
                dve.wait_ge(x_in, 16 * (p + 1))
                wait(dve, x1b_set, p)
                wait(dve, x4_in, 16 * NX4 * p)
                dve.tensor_tensor(x1[:], bP[:], xt[:], ALU.add).then_inc(x1_set, 1)

            def add_context(p):
                wait(dve, c_lo, p)
                for k in range(2):
                    dve.wait_ge(conv_mm, 2 * p + k + 1)
                    for b in range(2):
                        o = (2 * k + b) * 256
                        bias = ctxb[:, ds(p * P + b * NC, NC)].rearrange("p (h a o) -> p h a o", h=2, a=1)
                        for h in range(2):
                            op = dve.tensor_tensor(
                                ct[:, PH * k:PH * (k + 1), b * NC + h * HC:b * NC + (h + 1) * HC],
                                bC[:, o + h * P:o + (h + 1) * P].rearrange("p (q o) -> p q o", q=PH),
                                bias[:, h, :, :].broadcast_to([P, PH, HC]), ALU.add)
                    op.then_inc(conv_set, 1)

            def split_conv(p):
                dve.wait_ge(c_hi, p + 1)
                wait(dve, ffn_mm, p)
                dve.tensor_tensor(clo[:], ct[:], chi[:].bitcast(F32), ALU.subtract).then_inc(c_lo, 1)

            def router(p):
                base = ROUTE_ALL * p
                count = [0]

                def then(ins):
                    ins.then_inc(route, 1)
                    count[0] += 1
                    dve.wait_ge(route, base + count[0])

                dve.wait_ge(ffn_mm, p + 1)
                dve.tensor_copy(lg[:], bF[:, HID + P:HID + P + NE]).then_inc(route, 1)
                count[0] += 1
                then(dve.max(top[:], bF[:, HID + P:HID + P + NE]))
                dve.tensor_tensor(rs[:, 0:1], top[:, 1:2], top[:, 0:1], ALU.subtract).then_inc(route, 1)
                count[0] += 1
                assert count[0] == ROUTE_EXP
                then(dve.max_index(topi[:], top[:], lg[:]))
                then(dve.tensor_copy(rs[:, 4:6], topi[:, 0:2]))
                dve.wait_ge(route_exp, p + 1)
                then(dve.tensor_scalar(rs[:, 2:3], rs[:, 1:2], 1.0, None, ALU.add))
                then(dve.reciprocal(rs[:, 3:4], rs[:, 2:3]))
                then(dve.tensor_scalar(rs[:, 6:7], rs[:, 3:4], LORA_SCALE, None, ALU.mult))
                then(dve.tensor_tensor(rs[:, 7:8], rs[:, 1:2], rs[:, 6:7], ALU.mult))
                for k in range(2):
                    then(dve.tensor_scalar(we[:, k, :], iota[:], rs[:, 4 + k:5 + k], rs[:, 6 + k:7 + k],
                                           ALU.is_equal, ALU.mult))
                then(dve.tensor_tensor(we[:, 2, :], we[:, 0, :], we[:, 1, :], ALU.add))
                assert count[0] == ROUTE_ALL
                wait(dve, hw_tr, p)
                dve.tensor_tensor(hw[:].rearrange("p (e r) -> p e r", r=RANK),
                                  bF[:, HID:HID + P].rearrange("p (e r) -> p e r", r=RANK),
                                  we[:, 2, :].rearrange("p (e a) -> p e a", a=1).broadcast_to([P, NE, RANK]),
                                  ALU.mult).then_inc(hw_set, 1)

            def finish(p):
                dve.wait_ge(lora_mm, p + 1)
                dve.wait_ge(x1b_set, p + 1)
                wait(dve, stored, 16 * p)
                dve.tensor_tensor(osb[:, 0:2 * CW].rearrange("p (a c) -> p a c", a=2),
                                  bF[:, 0:1024].rearrange("p (a c) -> p a c", a=2)[:, :, 0:CW],
                                  x1b[:, 0:2 * CW].rearrange("p (a c) -> p a c", a=2), ALU.add)
                dve.tensor_tensor(osb[:, 2 * CW:L], bF[:, 1024:HID], x1b[:, 2 * CW:L], ALU.add).then_inc(out_set, 1)

            dve.wait_ge(consts, 16 * NCONST)
            for i in range(TOK // 512):
                cols = osb[:, (i % 2) * 512:(i % 2 + 1) * 512].rearrange("p (b o) -> p b o", o=NC)
                wait(dve, ctx_mm, i - 1)
                dve.tensor_tensor(cols, condT[:, 8 * i:8 * i + 8].rearrange("p (b a) -> p b a", a=1).broadcast_to([P, 8, NC]),
                                  cwT[:].rearrange("p (a o) -> p a o", a=1).broadcast_to([P, 8, NC]), ALU.mult
                                  ).then_inc(prods, 1)
                dve.wait_ge(ctx_mm, i + 1)
                dve.tensor_tensor(ctxb[:, 512 * i:512 * (i + 1)].rearrange("p (b o) -> p b o", o=NC),
                                  bC[:, (i % 2) * 512:(i % 2 + 1) * 512].rearrange("p (b o) -> p b o", o=NC),
                                  fside[:].rearrange("p (a o) -> p a o", a=1).broadcast_to([P, 8, NC]), ALU.add
                                  ).then_inc(ctx_set, 1)
            for i, (_, c, hi, lo, n) in enumerate(weights):
                dve.wait_ge(w_hi, i + 1)
                dve.tensor_tensor(lo[:, c, :], wst[i % NST][:, 0:n], hi[:, c, :].bitcast(F32), ALU.subtract
                                  ).then_inc(w_lo, 1)
                if i == 0:
                    split_y(0)
            dve.wait_ge(ctx_set, TOK // 512)

            def head():
                residual(0)
                split_y(1)
                residual(1)
                add_context(0)
                split_conv(0)

            def step(p, ahead):
                if ahead >= 2:
                    split_y(p + 2)
                router(p)
                finish(p)
                if ahead >= 1:
                    add_context(p + 1)
                    split_conv(p + 1)
                if ahead >= 2:
                    residual(p + 2)

            phases(dve, head, step)


ROUTE_EXP, ROUTE_ALL = 3, 12


def build(nc, d, out):
    y_dram = nc.dram_tensor("y_scratch", (NP, P, NG, P), F32).ap()
    with ExitStack() as ctx:
        with ExitStack() as front:
            bank = [front.enter_context(nc.psum_tensor(f"bank{i}", [P, 512], F32)) for i in range(8)]
            zhi = front.enter_context(nc.sbuf_tensor("z_hi", [P, KC, TOK], F32R))
            zlo = front.enter_context(nc.sbuf_tensor("z_lo", [P, KC, TOK], F32R))
            wst = front.enter_context(nc.sbuf_tensor("w_st", [P, KC, 3, P], F32))
            whi = front.enter_context(nc.sbuf_tensor("w_hi", [P, KC, 3, P], F32R))
            wlo = front.enter_context(nc.sbuf_tensor("w_lo", [P, KC, 3, P], F32R))
            w_in = front.enter_context(nc.semaphore("w_in"))
            w_his = {x: front.enter_context(nc.semaphore(f"w_hi_set{x}")) for x in (Q_, K_, V_)}
            w_los = {x: front.enter_context(nc.semaphore(f"w_lo_set{x}")) for x in (Q_, K_, V_)}
            weights = (wst, whi, wlo, whi[:, :, :, :].bitcast(F32), w_in, w_his, w_los)
            mix_phase(nc, d, bank, zhi, zlo, zhi[:, :, :].bitcast(F32), weights)
            attention_phase(nc, d, bank, zhi, zlo, y_dram, weights)
        bank2 = [ctx.enter_context(nc.psum_tensor(f"wide{i}", [P, 512 * n], F32)) for i, n in enumerate((2, 3, 2, 1))]
        ffn_phase(nc, d, bank2, y_dram, out)


def constants():
    theta = (1.0 / 10000.0 ** (np.arange(0, HD, 2, dtype=np.float32) / HD)).astype(np.float32)
    angle = np.outer(np.arange(NC, dtype=np.float32), theta).astype(np.float32)
    cos = np.cos(angle).astype(np.float32).T
    sin = np.sin(angle).astype(np.float32).T
    q, k = np.arange(P)[:, None] % NC, np.arange(NC)[None, :]
    return {
        "cos": np.tile(np.concatenate([cos, cos], 0), (GH, 1)),
        "sin": np.tile(np.concatenate([-sin, sin], 0), (GH, 1)),
        "mask": np.where(k <= q, 0.0, -1e30).astype(np.float32),
        "ident": np.eye(P, dtype=np.float32),
        "pick": np.repeat(np.eye(P // NM, dtype=np.float32), NM, 0),
        "iota": np.tile(np.arange(NE, dtype=np.float32), (P, 1)),
    }


def layouts(v):
    w = v["L0_cond2_weight"]
    toep = np.zeros((P, 6, P), np.float32)
    for h in range(2):
        for j in range(3):
            for f in range(PH):
                for q in range(PH):
                    tap = PH * (j - 1) + f - q + TAPS // 2
                    if 0 <= tap < TAPS:
                        for gr in range(HC // CG):
                            o = h * HC + gr * CG
                            toep[f * HC + gr * CG:f * HC + (gr + 1) * CG, 3 * h + j,
                                 q * HC + gr * CG:q * HC + (gr + 1) * CG] = w[o:o + CG, :, tap].T
    last = np.concatenate([v["L0_ffn_W_base"], v["L0_ffn_A"].reshape(NE * RANK, L), v["L0_ffn_W_router"]], 0)
    return {
        "x": v["x"],
        "condT": v["cond_128"].T,
        "W0": v["L0_cond_W0"], "W1": v["L0_cond_W1"], "W2": v["L0_cond_W2"],
        "b0": v["L0_cond_b0"][:, None], "b1": v["L0_cond_b1"][:, None], "b2": v["L0_cond_b2"][None],
        "mixw": v["L0_cond_weight"][..., 0].reshape(NM, OB, P // NM, NC).transpose(2, 0, 1, 3).reshape(P, OB, NC),
        "biask": v["L0_cond_bias_k"].reshape(NM, OB, P // NM).transpose(2, 0, 1).reshape(P, OB),
        "wqkvT": v["L0_attn_w_attn"].reshape(3, NG, P, KC, P).transpose(1, 4, 3, 0, 2),
        "wteT": v["L0_attn_adapter_wte"].reshape(NA, KC, P).transpose(2, 1, 0),
        "gate": np.broadcast_to(v["L0_attn_gating"], (P, 1)),
        "wprojT": v["L0_attn_w_proj"].T.reshape(KC, P, L),
        "wffnT": last.T.reshape(2, P, PH, NF).transpose(0, 2, 1, 3).reshape(KC, P, NF),
        "loraB": v["L0_ffn_B"].transpose(0, 2, 1).reshape(NE * RANK, L),
        "toep": toep,
        "bbase": np.broadcast_to(v["L0_ffn_b_base"], (P, L)),
        "cwT": v["L0_cond2_c_weight"].T,
        "fside": np.broadcast_to(v["fside_S_0"], (P, NC)),
    }


def kernel(**inputs):
    import concourse.bacc as bacc
    from concourse.bass_utils import run_bass_kernel_spmd as run

    nc = bacc.Bacc("TRN2", target_bir_lowering=False, num_devices=1, dynamic_dma_scratch_size=DMA_RING)
    arrays, d = {}, {}
    for name, a in {**layouts({k: np.asarray(a) for k, a in inputs.items()}), **constants()}.items():
        a = np.ascontiguousarray(a)
        arrays[f"in_{name}"] = a
        d[name] = nc.dram_tensor(f"in_{name}", a.shape, mybir.dt.from_np(a.dtype), kind="ExternalInput").ap()
    out = nc.dram_tensor("out_0", (NB, NC, L), F32, kind="ExternalOutput").ap()
    build(nc, d, out)
    r = run(nc, [arrays], core_ids=[0])
    return r.results[0]["out_0"]
```

```python
from contextlib import ExitStack

import numpy as np

import concourse.bass as bass
from concourse import mybir

F32 = mybir.dt.float32
F32R = mybir.dt.float32r
U32 = mybir.dt.uint32
ALU = mybir.AluOpType
ACT = mybir.ActivationFunctionType
AX = mybir.AxisListType.X
ds = bass.ds

P = 128
NB, NC, L = 32, 64, 1024
TOK = NB * NC
HD = 32
GH = P // HD
NG = L // P
UT = 512
NU = TOK // UT
UB = UT // NC
UP = UB // 2
KC = L // P
NP = NB // 2
NA = 10
NE, RANK = 8, 16
NM = 8
OB = NC * NM // P
TAPS, CG = 9, 16
PH = 8
CONV = NC // CG
NF = L + NE * RANK + NE
SCALE = 1.0 / float(np.sqrt(HD))
ASCALE = 1.0 / float(np.sqrt(L))
LORA_SCALE = 32 / RANK
HALF_SWAP = [(i + HD // 2) % HD for i in range(HD)]
Q_, K_, V_ = 0, 1, 2
MLP_COLS = (NB, P, 1, P, 1, NM, NC)
MIX_COLS = (OB * NC, OB, P // NM)
DMA_RING = 1024


def wait(eng, sem, value):
    if not isinstance(value, int) or value > 0:
        eng.wait_ge(sem, value)


def split_passes(hi_l, lo_l, hi_r, lo_r):
    return ((hi_l, hi_r), (hi_l, lo_r), (lo_l, hi_r))


class Space:

    def __init__(self, nc, prefix, at):
        self.nc, self.prefix, self.at = nc, prefix, at

    def take(self, name, shape, dt=F32):
        t = self.nc.alloc_sbuf_tensor_at(f"{self.prefix}_{name}", shape, dt, offset=self.at)
        self.at += -(-int(np.prod(shape[1:])) * 4 // 32) * 32
        return t


def split_columns(t, widths):
    ends = np.cumsum(widths)
    return [t[:, int(e - w):int(e)] for w, e in zip(widths, ends)]


def mixing(nc, ctx, d, psum, z, z_f, ctx_dram, first_weights, at):
    wst, whi, wlo, whi_f, w_in, w_hi, w_lo = first_weights
    NX = UP
    DC = 3
    bank = [psum[:, 512 * i:512 * (i + 1)] for i in range(8)]
    sb = Space(nc, "m", at).take

    def sem(name):
        return ctx.enter_context(nc.semaphore(name))

    mlp = sb("mlp", [P, sum(MLP_COLS)])
    condT, w0, b0, w1, b1, w2, cwT = split_columns(mlp, MLP_COLS)
    fside = sb("fside", [NB, NC])
    ctx_bias = sb("ctx_bias", [NB, NC])
    b2 = sb("b2", [1, NM])
    biask_wide = sb("biask_wide", [P, OB, P])
    ones = sb("ones", [1, NB])
    ident = sb("ident", [NB, NB])
    mix = sb("mix", [P, sum(MIX_COLS)])
    mixw, biask, pick = split_columns(mix, MIX_COLS)
    h0 = sb("h0", [P, NB])
    h1 = sb("h1", [P, NB])
    att = sb("att", [NB, NM])
    stat = sb("stat", [NB, 4])
    att_wide = sb("att_wide", [NB, P // NM, NM])
    att_sel = sb("att_sel", [P, 2, P // NM, NP])
    aggT = sb("aggT", [P, NP, 2, NC])
    aggb = sb("aggb", [P, TOK])
    xbuf = [sb(f"x{j}", [P, L]) for j in range(NX)]
    zt = [sb(f"z{j}", [P, KC, P]) for j in range(NX)]

    mlp_in = sem("m_mlp_in")
    consts = sem("m_consts")
    ones_set = sem("m_ones_set")
    ctx_mm = sem("m_ctx_mm")
    ctx_set = sem("m_ctx_set")
    ctx_out = sem("m_ctx_out")
    cleared = sem("m_cleared")
    mlp_mm = sem("m_mlp_mm")
    mlp_act = sem("m_mlp_act")
    soft = sem("m_soft")
    soft_exp = sem("m_soft_exp")
    bias_wide = sem("m_bias_wide")
    att_turned = sem("m_att_turned")
    att_spread = sem("m_att_spread")
    agg_mm = sem("m_agg_mm")
    agg_copied = sem("m_agg_copied")
    aggb_mm = sem("m_aggb_mm")
    aggb_copied = [sem(f"m_aggb_copied{k}") for k in range(2)]
    x_in = [sem(f"m_x_in{j}") for j in range(NX)]
    z_mm = [sem(f"m_z_mm{j}") for j in range(NX)]
    z_sum = [sem(f"m_z_sum{j}") for j in range(NX)]
    z_hi = [sem(f"m_z_hi{j}") for j in range(NX)]
    z_lo_dve = [sem(f"m_z_lo_dve{j}") for j in range(NX)]
    z_lo_pool = [sem(f"m_z_lo_pool{j}") for j in range(NX)]
    NCONST = 4
    zbank = [bank[6 - 2 * j:8 - 2 * j] for j in range(NX)]
    agg_psum, aggb_psum = bank[2:4], bank[0:2]

    def turns(eng, turn, between=None):
        turn(0)
        if between:
            between()
        with eng.Fori(1, NP // NX) as it:
            turn(it)

    def sync(sp):
        sp.dma_start(mlp[:], d["mlp"]).then_inc(mlp_in, 16)
        sp.dma_start(mix[:], d["mix"]).then_inc(consts, 16)
        sp.dma_start(fside[:], d["fside"]).then_inc(consts, 16)
        sp.dma_start(b2[:], d["b2"]).then_inc(consts, 16)
        sp.dma_start(ident[:], d["ident"][0:NB, 0:NB]).then_inc(consts, 16)
        for j in range(2):
            sp.dma_start(xbuf[j][:], d["x"][2 * j:2 * j + 2].rearrange("b c l -> (b c) l")).then_inc(x_in[j], 16)
        sp.dma_start(wst[:], d["wqkvT"][0]).then_inc(w_in, 16)
        for j in range(2, NX):
            sp.dma_start(xbuf[j][:], d["x"][2 * j:2 * j + 2].rearrange("b c l -> (b c) l")).then_inc(x_in[j], 16)
        sp.wait_ge(ctx_set, 1)
        sp.dma_start(ctx_dram.rearrange("a (b o) -> (a b) o", o=NC), ctx_bias[:]).then_inc(ctx_out, 16)
        with sp.Fori(1, NP // NX) as it:
            for j in range(NX):
                sp.wait_ge(z_mm[j], it)
                sp.dma_start(xbuf[j][:], d["x"][ds((it * NX + j) * 2, 2)].rearrange("b c l -> (b c) l")
                             ).then_inc(x_in[j], 16)

    def tensor(pe):
        pe.wait_ge(mlp_in, 16)
        pe.matmul(bank[0][:, 0:NB], w0, condT, start=True, stop=True).then_inc(mlp_mm, 1)
        pe.matmul(bank[1][0:NB, 2 * NB:2 * NB + NC], condT, cwT, start=True, stop=True).then_inc(ctx_mm, 1)
        pe.wait_ge(mlp_act, 1)
        pe.matmul(bank[0][:, 64:64 + NB], w1, h0[:], start=True, stop=True).then_inc(mlp_mm, 1)
        pe.wait_ge(mlp_act, 2)
        pe.wait_ge(consts, 16 * NCONST)
        pe.wait_ge(ones_set, 1)
        pe.matmul(bank[0][0:NB, 128:128 + NM], h1[:], w2, start=True, stop=False)
        pe.matmul(bank[0][0:NB, 128:128 + NM], ones[0:1, 0:NB], b2[:], start=False, stop=True).then_inc(mlp_mm, 1)
        pe.wait_ge(soft, 5)
        pe.matmul(bank[1][:, 0:NB], att_wide[:].rearrange("b o k -> b (o k)"), ident[:], start=True, stop=True
                  ).then_inc(att_turned, 1)
        pe.wait_ge(att_spread, 1)
        for n in range(OB):
            for b in range(2):
                mm = pe.matmul(agg_psum[n // 2][NC * b:NC * (b + 1), 256 * (n % 2):256 * (n % 2 + 1)],
                               mixw[:, n * NC:(n + 1) * NC], att_sel[:, b, :, :].rearrange("p o i -> p (o i)"),
                               start=True, stop=True)
            if n % 2:
                mm.then_inc(agg_mm, 1)
        pe.wait_ge(bias_wide, 1)
        for n in range(OB):
            wait(pe, aggb_copied[n % 2], n // 2)
            pe.matmul(aggb_psum[n % 2][:], biask_wide[:, n, :], att_sel[:].rearrange("p b o i -> p (b o i)"),
                      start=True, stop=True).then_inc(aggb_mm, 1)
        pe.wait_ge(agg_copied, 4)

        def turn(it):
            for j in range(NX):
                pe.wait_ge(x_in[j], 16 * it + 16)
                if isinstance(it, int) and j == NX - 1:
                    for k in range(2):
                        pe.wait_ge(aggb_copied[k], 2)
                wait(pe, z_sum[j], it)
                for c in range(KC):
                    mm = pe.matmul(zbank[j][c // 4][:, (c % 4) * P:(c % 4 + 1) * P],
                                   xbuf[j][:, c * P:(c + 1) * P],
                                   aggT[:, ds(it * NX + j, 1), :, :].rearrange("p a b o -> p (a b o)"),
                                   start=True, stop=True)
                mm.then_inc(z_mm[j], 1)

        turns(pe, turn)

    def z_place(z, it, j, part, c0, c1):
        return z[:, ds(it, 1), part, c0:c1, j * P:(j + 1) * P].rearrange("p a c t -> p (a c) t")

    def agg_copy(copy, q, b):
        return copy(aggT[NC * b:NC * (b + 1), :, b, 32 * q:32 * q + 32].rearrange("p b o -> p o b"),
                    agg_psum[q][NC * b:NC * (b + 1), :].rearrange("p (o b) -> p o b", b=NP))

    def bias_copy(copy, n):
        o = P // NM
        return copy(aggb[:].rearrange("p (i b o) -> p b o i", b=2, o=NC)[:, :, n * o:(n + 1) * o, :],
                    aggb_psum[n % 2][:].rearrange("p (b o i) -> p b o i", b=2, i=NP))

    def scalar(act):
        for n, (h, b) in enumerate(((h0, b0), (h1, b1))):
            act.wait_ge(mlp_mm, n + 1)
            act.activation(h[:], bank[0][:, 64 * n:64 * n + NB], ACT.Gelu, bias=b[:, 0:1]).then_inc(mlp_act, 1)
        act.wait_ge(soft, 2)
        act.activation(att[:], att[:], ACT.Exp).then_inc(soft_exp, 1)
        act.wait_ge(agg_mm, 1)
        act.wait_ge(cleared, 1)
        for b in range(2):
            agg_copy(lambda o, i: act.activation(o, i, ACT.Copy), 0, b).then_inc(agg_copied, 1)
        for n in range(1, OB, 2):
            act.wait_ge(aggb_mm, n + 1)
            bias_copy(lambda o, i: act.activation(o, i, ACT.Copy), n).then_inc(aggb_copied[1], 1)

        def split_weights():
            act.wait_ge(w_in, 16)
            for x in (K_, Q_, V_):
                act.activation(whi[:, :, x, :], wst[:, :, x, :], ACT.Copy).then_inc(w_hi[x], 1)

        def turn(it):
            for j in range(NX):
                act.wait_ge(z_sum[j], it + 1)
                act.activation(z_place(z, it, j, 0, 0, KC), zt[j][:], ACT.Copy).then_inc(z_hi[j], 1)

        turns(act, turn, split_weights)

    def z_lo(eng, it, j, c0, c1):
        return eng.tensor_tensor(z_place(z, it, j, 1, c0, c1), zt[j][:, c0:c1, :], z_place(z_f, it, j, 0, c0, c1),
                                 ALU.subtract)

    def gpsimd(pool):
        pool.memset(aggT[:], 0.0).then_inc(cleared, 1)

        def turn(it):
            for j in range(NX):
                pool.wait_ge(z_hi[j], it + 1)
                z_lo(pool, it, j, DC, KC).then_inc(z_lo_pool[j], 1)

        turns(pool, turn)

    def vector(dve):
        dve.memset(ones[:], 1.0).then_inc(ones_set, 1)
        dve.wait_ge(consts, 16 * NCONST)
        dve.tensor_copy(biask_wide[:], biask.rearrange("p (n a) -> p n a", a=1).broadcast_to([P, OB, P])
                        ).then_inc(bias_wide, 1)
        dve.wait_ge(ctx_mm, 1)
        dve.tensor_tensor(ctx_bias[:], bank[1][0:NB, 2 * NB:2 * NB + NC], fside[:], ALU.add).then_inc(ctx_set, 1)
        dve.wait_ge(mlp_mm, 3)
        dve.reduce_max(stat[:, 0:1], bank[0][0:NB, 128:128 + NM], AX).then_inc(soft, 1)
        dve.wait_ge(soft, 1)
        dve.tensor_scalar(att[:], bank[0][0:NB, 128:128 + NM], stat[:, 0:1], None, ALU.subtract).then_inc(soft, 1)
        dve.wait_ge(soft_exp, 1)
        dve.reduce_sum(stat[:, 1:2], att[:], AX).then_inc(soft, 1)
        dve.wait_ge(soft, 3)
        dve.reciprocal(stat[:, 2:3], stat[:, 1:2]).then_inc(soft, 1)
        dve.wait_ge(soft, 4)
        dve.tensor_scalar(att_wide[:], att[:].rearrange("b (a k) -> b a k", a=1).broadcast_to([NB, P // NM, NM]),
                          stat[:, 2:3], None, ALU.mult).then_inc(soft, 1)
        dve.wait_ge(att_turned, 1)
        dve.tensor_tensor(
            att_sel[:],
            bank[1][:, 0:NB].rearrange("p (i b a) -> p b a i", b=2, a=1).broadcast_to([P, 2, P // NM, NP]),
            pick.rearrange("p (b o a) -> p b o a", b=1, a=1).broadcast_to([P, 2, P // NM, NP]), ALU.mult
            ).then_inc(att_spread, 1)
        dve.wait_ge(agg_mm, 2)
        dve.wait_ge(cleared, 1)
        for b in range(2):
            agg_copy(dve.tensor_copy, 1, b).then_inc(agg_copied, 1)
        for n in range(0, OB, 2):
            dve.wait_ge(aggb_mm, n + 1)
            bias_copy(dve.tensor_copy, n).then_inc(aggb_copied[0], 1)
        for k in range(2):
            dve.wait_ge(aggb_copied[k], 2)

        def split_weights(names):
            for x in names:
                dve.wait_ge(w_hi[x], 1)
                dve.tensor_tensor(wlo[:, :, x, :], wst[:, :, x, :], whi_f[:, :, x, :], ALU.subtract
                                  ).then_inc(w_lo[x], 1)

        def make_lo(it, j):
            dve.wait_ge(z_hi[j], it + 1)
            z_lo(dve, it, j, 0, DC).then_inc(z_lo_dve[j], 1)

        def turn(it):
            for j in range(NX):
                dve.wait_ge(z_mm[j], it + 1)
                wait(dve, z_lo_pool[j], it)
                wait(dve, z_lo_dve[j], it)
                for half in range(2):
                    z = dve.tensor_tensor(
                        zt[j][:, 4 * half:4 * half + 4, :],
                        zbank[j][half][:].rearrange("p (c t) -> p c t", t=P),
                        aggb[:, ds((it * NX + j) * P, P)].rearrange("p (a t) -> p a t", a=1).broadcast_to([P, 4, P]),
                        ALU.add)
                z.then_inc(z_sum[j], 1)
                if j >= 1:
                    make_lo(it, j - 1)
                elif not isinstance(it, int):
                    make_lo(it - 1, NX - 1)

        turns(dve, turn, lambda: split_weights((K_,)))
        make_lo(NP // NX - 1, NX - 1)
        split_weights((Q_, V_))

    return (sync, gpsimd, tensor, scalar, vector), ctx_out, z_sum, z_lo_dve, z_lo_pool


def program(nc, d, psum, z, zbase, y_dram, x1_dram, ctx_dram, weights, out):
    wst, whi, wlo, whi_f, w_in, w_hi, w_lo = weights
    bank = [psum[:, 512 * i:512 * (i + 1)] for i in range(8)]
    with ExitStack() as ctx:
        def sem(name):
            return ctx.enter_context(nc.semaphore(name))

        Z = 2 * KC * UT * 4
        front = Space(nc, "f", zbase)
        wp_raw = front.take("wp_raw", [P, KC, L])
        wphi = front.take("wphi", [P, KC, L], F32R)
        wplo = front.take("wplo", [P, KC, L], F32R)
        wfhi = front.take("wfhi", [P, KC, NF], F32R)
        wflo = front.take("wflo", [P, KC, NF], F32R)
        over = Space(nc, "f", zbase)
        yst = over.take("yst", [P, KC, P])
        yhi = over.take("yhi", [P, KC, P], F32R)
        ylo = over.take("ylo", [P, KC, P], F32R)
        xt = over.take("xt", [P, L])
        x1 = over.take("x1", [P, L])
        raw0 = Space(nc, "f", over.at).take("wf_raw0", [P, NF])
        x1b = over.take("x1b", [P, L])
        osb = over.take("osb", [P, L])
        ct = over.take("ct", [P, KC, P])
        assert over.at == zbase + Z

        adapters_at = zbase + NU * Z + 3 * KC * 3 * P * 4
        adapters = Space(nc, "a", adapters_at)
        wte2 = adapters.take("wte2", [P, KC * 2 * NA + P - 2 * NA], F32R)
        wte2_parts = wte2[:, 0:KC * 2 * NA].rearrange("p (c b a) -> p c b a", b=2, a=NA)
        adapters.at = max(adapters.at, front.at)

        both = Space(nc, "", adapters.at)
        ident = both.take("ident", [P, P])
        loraB = both.take("loraB", [P, L])
        toep = both.take("toep", [P, CONV, 2, P])
        iota = both.take("iota", [P, NE])
        x8 = both.take("x8", [P, 2 * CONV, L // PH + 1])

        attn = Space(nc, "a", both.at)
        sb = attn.take
        kbd = sb("kbd", [P, UB, GH, NC])
        qr = sb("qr", [P, UT])
        kr = sb("kr", [P, UT])
        rot = sb("rot", [P, UT])
        wte = sb("wte", [P, KC, NA])
        cosT = sb("cos", [P, NC])
        sinT = sb("sin", [P, NC])
        mask = sb("mask", [P, NC])
        gate = sb("gate", [P, 1])
        vT = sb("vT", [P, UT])
        vbd = sb("vbd", [P, UP, 2, 2, 2 * HD])
        prob = [sb(f"prob{t}", [P, 8, NC]) for t in range(2)]
        pT = [sb(f"pT{t}", [P, 2, 2, P]) for t in range(2)]
        stat = sb("stat", [P, 2, 3, 8])
        aprob = sb("aprob", [P, UP, P], F32R)
        atmp = sb("atmp", [P, UP * GH, NA])
        astat = sb("astat", [P, 3, UP * GH])
        aT = sb("aT", [P, UT], F32R)
        akv = sb("akv", [2 * NA, 2 * P])
        akbd = sb("akbd", [P, GH, NA])
        avbd = sb("avbd", [P, P], F32R)
        avs = sb("avs", [P, P])
        avh = sb("avh", [P, P], F32R)
        asel = sb("asel", [2 * NA, P])
        afold = sb("afold", [2 * NA, NA])
        alow = sb("alow", [P, 1])
        amask = sb("amask", [P, P])
        ysb = sb("ysb", [P, UT])

        pairs = Space(nc, "f", both.at)
        sb = pairs.take
        raw2 = Space(nc, "f", both.at).take("wf_raw2", [P, NF])
        chi = sb("chi", [P, KC, P], F32R)
        clo = sb("clo", [P, KC, P], F32R)
        assert pairs.at == both.at + UB * GH * NC * 4
        raw1 = sb("wf_raw1", [P, NF])
        hw = sb("hw", [P, P])
        hwThi = sb("hwThi", [P, P], F32R)
        hwTlo = sb("hwTlo", [P, P], F32R)
        lg = sb("lg", [P, NE])
        top = sb("top", [P, 8])
        topi = sb("topi", [P, 8], U32)
        rs = sb("rs", [P, 8])
        we = sb("we", [P, 3, NE])
        ctxb = sb("ctxb", [P, TOK])
        bbase = sb("bbase", [P, L])
        loraBhi = sb("loraBhi", [P, L], F32R)
        loraBlo = sb("loraBlo", [P, L], F32R)
        assert attn.at <= nc.sbuf_usable_end and pairs.at <= nc.sbuf_usable_end
        NST = 3
        wf_raw = [raw0[:], raw1[:], raw2[:]]
        PL = 5
        WF_DVE = (2, 5, 7)

        bS, bPT, bY, bAD, bQ, bK, bV = bank[0:2], bank[2], bank[3], bank[4], bank[5], bank[6], bank[7]
        AKT, AVS = 2 * P, 3 * P
        AR = GH * NA
        bF, bC, bP, bT = psum[:, 0:3 * 512], psum[:, 3 * 512:5 * 512], psum[:, 5 * 512:7 * 512], psum[:, 7 * 512:8 * 512]
        CW = 388
        cuts = [(512 * i, CW * i, min(CW * (i + 1), NF)) for i in range(3)]
        HID = 512 * 2 + L - 2 * CW

        consts = sem("a_consts")
        cleared = sem("a_cleared")
        wte_hi = sem("a_wte_hi")
        wte_lo = sem("a_wte_lo")
        mm_done = {Q_: sem("a_q_mm"), K_: sem("a_k_mm"), V_: sem("a_v_mm")}
        turned = {Q_: sem("a_q_turned"), K_: sem("a_k_turned")}
        rotated = {Q_: sem("a_q_rotated"), K_: sem("a_k_rotated")}
        rot_step = sem("a_rot_step")
        kbd_set = sem("a_kbd_set")
        vT_copied = sem("a_vT_copied")
        v_tr = sem("a_v_tr")
        vbd_set = sem("a_vbd_set")
        scores = sem("a_scores")
        masked = sem("a_masked")
        row_max = sem("a_row_max")
        shifted = sem("a_shifted")
        exped = sem("a_exped")
        row_sum = sem("a_row_sum")
        inverted = sem("a_inverted")
        probs = sem("a_probs")
        p_tr = sem("a_p_tr")
        pT_copied = sem("a_pT_copied")
        ascores = sem("a_ascores")
        amax = sem("a_amax")
        ashifted = sem("a_ashifted")
        aexped = sem("a_aexped")
        asum = sem("a_asum")
        ainv = sem("a_ainv")
        agated = sem("a_agated")
        aprobs = sem("a_aprobs")
        a_tr = sem("a_a_tr")
        aT_copied = sem("a_aT_copied")
        akv_mm = sem("a_akv_mm")
        akv_copied = sem("a_akv_copied")
        avs_set = sem("a_avs_set")
        avh_set = sem("a_avh_set")
        aweighted = sem("a_aweighted")
        aprob_hi = sem("a_aprob_hi")
        ak_tr = sem("a_ak_tr")
        akbd_set = sem("a_akbd_set")
        avbd_set = sem("a_avbd_set")
        y_mm = sem("a_y_mm")
        y_copied = sem("a_y_copied")
        y_out = sem("a_y_out")
        NCONST, NCLEAR, NFCONST = 10, 5, 3

        fconsts = sem("f_consts")
        edges = sem("f_edges")
        wp_in = sem("f_wp_in")
        wp_hi = sem("f_wp_hi")
        wp_lo_pool = sem("f_wp_lo_pool")
        wp_lo_dve = sem("f_wp_lo_dve")
        wf_in = [sem(f"f_wf_in{i}") for i in range(NST)]
        wf_hi_set = sem("f_wf_hi")
        wf_lo_pool = sem("f_wf_lo_pool")
        wf_lo_dve = sem("f_wf_lo_dve")
        ctxb_in = sem("f_ctxb_in")
        y_in = sem("f_y_in")
        y_hi = sem("f_y_hi")
        y_lo = sem("f_y_lo")
        x_in = sem("f_x_in")
        proj_mm = sem("f_proj_mm")
        x1_set = sem("f_x1_set")
        x1b_set = sem("f_x1b_set")
        x1_out = sem("f_x1_out")
        bbase_in = sem("f_bbase_in")
        x8_in = sem("f_x8_in")
        conv_mm = sem("f_conv_mm")
        conv_set = sem("f_conv_set")
        c_hi = sem("f_c_hi")
        c_lo = sem("f_c_lo")
        ffn_mm = sem("f_ffn_mm")
        hidden_mm = sem("f_hidden_mm")
        route = sem("f_route")
        route_exp = sem("f_route_exp")
        hw_set = sem("f_hw_set")
        hw_tr = sem("f_hw_tr")
        lora_hi = sem("f_lora_hi")
        lora_lo = sem("f_lora_lo")
        hwT_hi = sem("f_hwT_hi")
        hwT_set = sem("f_hwT_set")
        lora_mm = sem("f_lora_mm")
        hidden_free = sem("f_hidden_free")
        out_set = sem("f_out_set")
        stored = sem("f_stored")
        bank_free = (out_set, out_set, hidden_free)

        parts, ctx_out, z_sum, z_lo_dve, z_lo_pool = mixing(
            nc, ctx, d, psum, z, z[:, :, :, :, :].bitcast(F32), ctx_dram, weights, adapters_at)
        mix_sync, mix_gpsimd, mix_tensor, mix_scalar, mix_vector = parts

        def wait_z(eng, units):
            eng.wait_ge(z_lo_pool[UP - 1], units)
            eng.wait_ge(z_lo_dve[UP - 1], units)

        block = ctx.enter_context(nc.Block())

        def unit_steps(eng, step):
            def turn(g):
                for u in range(NU // 2, NU):
                    step(g, u)
                for u in range(NU // 2):
                    step(g + 1, u)

            for u in range(NU // 2):
                step(0, u)
            with eng.Fori(0, NG - 2) as g:
                turn(g)
            turn(NG - 2)
            for u in range(NU // 2, NU):
                step(NG - 1, u)

        def first(g, u):
            return isinstance(g, int) and g == 0 and u == 0

        def last(g):
            return isinstance(g, int) and g == NG - 1

        def refill(g, u):
            return u == NU - 1 and not last(g)

        def pair_steps(eng, step):
            step(0, 3)
            with eng.Fori(1, NP - 3) as p:
                step(p, 3)
            for p in range(NP - 3, NP):
                step(p, NP - 1 - p)

        def wf_lo_count(i):
            made = [k for k in range(i + 1) if (k in WF_DVE) == (i in WF_DVE)]
            return (wf_lo_dve if i in WF_DVE else wf_lo_pool), len(made)

        @block.sync
        def _(sp):
            mix_sync(sp)
            wait_z(sp, NU)
            for dst, src in ((wte, "wteT"), (cosT, "cos"), (sinT, "sin"), (mask, "mask"), (ident, "ident"),
                             (gate, "gate"), (asel, "asel"), (amask, "amask"), (afold, "afold"), (alow, "alow")):
                sp.dma_start(dst[:], d[src]).then_inc(consts, 16)
            for dst, src in ((iota, "iota"), (loraB, "loraB"), (toep, "toep")):
                sp.dma_start(dst[:], d[src]).then_inc(fconsts, 16)

            def store_y(g, u):
                sp.wait_ge(y_copied, NU * g + u + 1)
                sp.dma_start(y_dram[u * UP:(u + 1) * UP, :, ds(g, 1), :].rearrange("i p a t -> p i (a t)"),
                             ysb[:].rearrange("p (i t) -> p i t", i=UP)).then_inc(y_out, 16)

            def load_wf(i):
                if i >= NST:
                    sp.wait_ge(*wf_lo_count(i - NST))
                sp.dma_start(wf_raw[i % NST], d["wffnT"][i]).then_inc(wf_in[i % NST], 16)

            def load_y(p):
                wait(sp, y_lo, p)
                sp.dma_start(yst[:], y_dram[ds(p, 1)].rearrange("a p k t -> p (a k) t")).then_inc(y_in, 16)

            def load_x(p):
                wait(sp, x1_set, p)
                sp.dma_start(xt[:], d["x"][ds(p * 2, 2)].rearrange("b c l -> (b c) l")).then_inc(x_in, 16)

            def early(u):
                if u == 1:
                    sp.wait_ge(mm_done[V_], NU * (NG - 1) + 1)
                    for c in range(KC):
                        sp.dma_start(wp_raw[:, c, :], d["wprojT"][c]).then_inc(wp_in, 16)
                if u == NU - 1:
                    sp.wait_ge(wp_lo_pool, PL)
                    sp.wait_ge(y_out, 16 * (NU * (NG - 1) + 1))
                    load_y(0)
                    load_x(0)
                    sp.wait_ge(wp_lo_dve, KC - PL)
                    load_wf(0)

            def unit_step(g, u):
                if last(g):
                    early(u)
                if not first(g, u):
                    store_y(*((g, u - 1) if u else (g - 1, NU - 1)))
                if u == 2 and not last(g):
                    for x in (Q_, K_, V_):
                        sp.wait_ge(w_lo[x], g + 1)
                    sp.dma_start(wst[:], d["wqkvT"][ds(g + 1, 1)].rearrange("a p k x c -> p (a k) x c")
                                 ).then_inc(w_in, 16)

            def put_aside(p):
                sp.wait_ge(x1_set, p + 1)
                sp.dma_start(x1_dram[ds(p, 1)].rearrange("a t l -> (a t) l"), x1[:]).then_inc(x1_out, 16)

            def spread(p):
                sp.wait_ge(x1_out, 16 * (p + 1))
                wait(sp, conv_mm, 2 * p)
                for f in range(PH):
                    q, u = (f - TAPS // 2) % PH, int(f < TAPS // 2)
                    sp.dma_start(x8[CG * f:CG * (f + 1), :, u:u + L // PH],
                                 x1_dram[ds(p, 1)].rearrange("a (g c) (q m) -> (a c) g q m", c=CG, q=PH)[:, :, q, :]
                                 ).then_inc(x8_in, 16)

            def store_out(p):
                sp.wait_ge(out_set, p + 1)
                sp.dma_start(out[ds(p * 2, 2)].rearrange("b c l -> (b c) l"), osb[:]).then_inc(stored, 16)

            unit_steps(sp, unit_step)
            sp.wait_ge(scores, 2 * NG * NU)
            sp.wait_ge(ascores, NG * NU)
            for i in range(1, NST + 1):
                load_wf(i)
            load_y(1)
            for i in range(NST + 1, 2 * NST):
                load_wf(i)
            put_aside(0)
            load_wf(2 * NST)
            store_y(NG - 1, NU - 1)
            sp.wait_ge(ctx_out, 16)
            sp.dma_start(ctxb[:], ctx_dram.broadcast_to([P, TOK])).then_inc(ctxb_in, 16)
            spread(0)
            load_wf(KC - 1)
            load_x(1)
            sp.wait_ge(y_out, 16 * NG * NU)
            sp.dma_start(bbase[:], d["bbase"]).then_inc(bbase_in, 16)
            load_y(2)
            put_aside(1)
            spread(1)

            def pair_step(p, ahead):
                if ahead >= 2:
                    load_x(p + 2)
                if ahead >= 3:
                    load_y(p + 3)
                store_out(p)
                if ahead >= 2:
                    put_aside(p + 2)
                    spread(p + 2)

            pair_steps(sp, pair_step)
            sp.wait_ge(stored, 16 * NP)

        @block.gpsimd
        def _(pool):
            mix_gpsimd(pool)
            wait_z(pool, NU)
            for t in (kbd, vbd, akbd):
                pool.memset(t[:], 0.0).then_inc(cleared, 1)
            for t in (wte2, aprob):
                pool.memset(t[:].bitcast(F32), 0.0).then_inc(cleared, 1)

            pool.wait_ge(mm_done[V_], NU * NG - 1)
            for c in range(PL):
                pool.wait_ge(wp_hi, c + 1)
                pool.tensor_tensor(wplo[:, c, :], wp_raw[:, c, :], wphi[:, c, :].bitcast(F32), ALU.subtract
                                   ).then_inc(wp_lo_pool, 1)
            for i in range(KC):
                if i not in WF_DVE:
                    pool.wait_ge(wf_hi_set, i + 1)
                    pool.tensor_tensor(wflo[:, i, :], wf_raw[i % NST], wfhi[:, i, :].bitcast(F32), ALU.subtract
                                       ).then_inc(wf_lo_pool, 1)
            pool.wait_ge(fconsts, 16 * NFCONST)

            def add_bias(p):
                pool.wait_ge(x1_set, p + 1)
                wait(pool, out_set, p)
                pool.tensor_tensor(x1b[:].rearrange("p (m q) -> p q m", q=PH), x1[:].rearrange("p (q m) -> p q m", q=PH),
                                   bbase[:].rearrange("p (m q) -> p q m", q=PH), ALU.add).then_inc(x1b_set, 1)

            def pair_step(p, ahead):
                if ahead >= 1:
                    add_bias(p + 1)

            pool.wait_ge(wf_lo_pool, KC - len(WF_DVE))
            pool.wait_ge(bbase_in, 16)
            add_bias(0)
            pair_steps(pool, pair_step)

        @block.tensor
        def _(pe):
            mix_tensor(pe)
            def attend_scores(m):
                pe.wait_ge(rotated[Q_], m + 1)
                pe.wait_ge(kbd_set, m + 1)
                wait(pe, aT_copied, m)
                wait(pe, pT_copied, 2 * m)
                for s in range(UP):
                    for b in range(2):
                        mm = pe.matmul(bS[s // 2][NC * b:NC * b + NC, (s % 2) * GH * NC:(s % 2 + 1) * GH * NC],
                                       qr[:, (2 * s + b) * NC:(2 * s + b + 1) * NC],
                                       kbd[:, 2 * s + b, :, :].rearrange("p h k -> p (h k)"), start=True, stop=True)
                    if s % 2:
                        mm.then_inc(scores, 1)

            def attend_ascores(m, groups):
                wait(pe, ashifted, m)
                pe.wait_ge(akbd_set, groups)
                for i in range(UP):
                    for b in range(2):
                        mm = pe.matmul(bAD[NC * b:NC * (b + 1), i * GH * NA:(i + 1) * GH * NA],
                                       qr[:, (2 * i + b) * NC:(2 * i + b + 1) * NC],
                                       akbd[:].rearrange("p h a -> p (h a)"), start=True, stop=True)
                mm.then_inc(ascores, 1)

            def attend_transposes(m):
                pe.wait_ge(aprobs, m + 1)
                for i in range(UP):
                    tr = pe.transpose(bS[0][:, i * P:(i + 1) * P], aprob[:, i, :].bitcast(F32),
                                      ident[:])
                tr.then_inc(a_tr, 1)
                wait(pe, pT_copied, 2 * m)
                for t, dst in ((0, bPT), (1, bS[1])):
                    pe.wait_ge(probs, 2 * m + t + 1)
                    for j in range(4):
                        tr = pe.transpose(dst[:, j * P:(j + 1) * P],
                                          prob[t][:, 2 * j:2 * j + 2, :].rearrange("p h k -> p (h k)"), ident[:])
                    tr.then_inc(p_tr, 1)

            def attend_values(m, groups):
                pe.wait_ge(aT_copied, m + 1)
                pe.wait_ge(avbd_set, groups)
                wait(pe, y_copied, m)
                pe.matmul(bY[:], avbd[:], aT[:], start=True, stop=True)
                pe.wait_ge(vbd_set, m + 1)
                for s in range(UP):
                    if s % 2 == 0:
                        pe.wait_ge(pT_copied, 2 * m + s // 2 + 1)
                    for b in range(2):
                        for hp in range(2):
                            mm = pe.matmul(bY[2 * HD * hp:2 * HD * (hp + 1), (2 * s + b) * NC:(2 * s + b + 1) * NC],
                                           vbd[:, s, b, hp, :], pT[s // 2][:, s % 2, hp, NC * b:NC * b + NC],
                                           start=False, stop=True, skip_group_check=True)
                mm.then_inc(y_mm, 1)

            def project_qkv(x, dst, g, u):
                pe.wait_ge(w_lo[x], g + 1)
                for c in range(KC):
                    for i, (w, zs) in enumerate(split_passes(whi, wlo, z[:, u, 0, c, :], z[:, u, 1, c, :])):
                        mm = pe.matmul(dst, w[:, c, x, :], zs,
                                       start=(c == 0 and i == 0), stop=(c == KC - 1 and i == 2))
                mm.then_inc(mm_done[x], 1)

            def unit_step(g, u):
                n = NU * g + u
                groups = g + 1 if u else g
                att = not first(g, u)
                if isinstance(g, int) and g == 0:
                    wait_z(pe, u + 1 if u == 0 else NU)
                if not att:
                    for j in range(2):
                        pe.wait_ge(z_sum[j], NP // UP)
                if att:
                    attend_scores(n - 1)
                    attend_ascores(n - 1, groups)
                wait(pe, turned[K_], n)
                project_qkv(K_, bK, g, u)
                wait(pe, turned[Q_], n)
                project_qkv(Q_, bQ, g, u)
                if att:
                    attend_transposes(n - 1)
                wait(pe, vbd_set, n)
                project_qkv(V_, bV, g, u)
                if u == 0:
                    pe.wait_ge(wte_lo, 1)
                    wait(pe, ashifted, n)
                    for c in range(KC):
                        for i, w in enumerate((whi, wlo)):
                            mm = pe.matmul(bAD[:, 0:2 * P], wte2[:, c * 2 * NA:c * 2 * NA + P],
                                           w[:, c, K_:V_ + 1, :].rearrange("p x c -> p (x c)"),
                                           start=(c == 0 and i == 0), stop=(c == KC - 1 and i == 1))
                    mm.then_inc(akv_mm, 1)
                if att:
                    attend_values(n - 1, groups)
                if u == 0:
                    pe.wait_ge(akv_copied, g + 1)
                pe.wait_ge(vT_copied, n + 1)
                for i in range(UP):
                    tr = pe.transpose(bV[:, i * P:(i + 1) * P], vT[:, i * P:(i + 1) * P], ident[:])
                tr.then_inc(v_tr, 1)
                if u == 0:
                    pe.matmul(bAD[:, AVS:AVS + P], asel[:], akv[:, P:2 * P], start=True, stop=True)
                    pe.matmul(bAD[:, AKT:AKT + NA], akv[:, 0:P], afold[:], start=True, stop=True).then_inc(ak_tr, 1)

            def project_out(p, c0, c1):
                if c0 == 0:
                    pe.wait_ge(y_lo, p + 1)
                    wait(pe, x1_set, p)
                for c in range(c0, c1):
                    for i, (y, w) in enumerate(split_passes(yhi, ylo, wphi, wplo)):
                        for n in range(2):
                            mm = pe.matmul(bP[:, n * 512:(n + 1) * 512], y[:, c, :], w[:, c, n * 512:(n + 1) * 512],
                                           start=(c == 0 and i == 0), stop=(c == KC - 1 and i == 2))
                if c1 == KC:
                    mm.then_inc(proj_mm, 1)

            def convolve(p):
                pe.wait_ge(x8_in, 16 * PH * (p + 1))
                wait(pe, conv_set, 2 * p)
                for b in range(2):
                    for g in range(CONV):
                        for j in range(2):
                            o = 512 * b + P * g
                            mm = pe.matmul(bC[:, o:o + P], x8[:, CONV * b + g, j:j + P], toep[:, g, j, :],
                                           start=(j == 0), stop=(j == 1))
                    mm.then_inc(conv_mm, 1)

            def last_layer(p, columns, c):
                if isinstance(p, int) and p == 0:
                    pe.wait_ge(*wf_lo_count(c))
                if c == 0:
                    pe.wait_ge(c_lo, 2 * (p + 1))
                for i, (a, w) in enumerate(split_passes(chi, clo, wfhi, wflo)):
                    for k in columns:
                        if c == 0 and i == 0:
                            wait(pe, bank_free[k], p)
                        at, n0, n1 = cuts[k]
                        mm = pe.matmul(bF[:, at:at + n1 - n0], a[:, c, :], w[:, c, n0:n1],
                                       start=(c == 0 and i == 0), stop=(c == KC - 1 and i == 2))
                        if c == KC - 1 and i == 2 and k == 2:
                            mm.then_inc(hidden_mm, 1)
                        if c == KC - 1 and i == 2 and k == 1:
                            mm.then_inc(ffn_mm, 1)

            def turn_hidden(p):
                pe.wait_ge(hw_set, p + 1)
                wait(pe, hwT_set, p)
                pe.transpose(bT[:, 0:P], hw[:], ident[:]).then_inc(hw_tr, 1)

            def low_rank(p):
                if isinstance(p, int) and p == 0:
                    pe.wait_ge(lora_lo, 1)
                pe.wait_ge(hwT_set, p + 1)
                for k in (2, 0, 1):
                    at, n0, n1 = cuts[k]
                    n1 = min(n1, L)
                    for h, w in split_passes(hwThi, hwTlo, loraBhi, loraBlo):
                        mm = pe.matmul(bF[:, at:at + n1 - n0], h[:], w[:, n0:n1],
                                       start=False, stop=True, skip_group_check=True)
                    if k != 0:
                        mm.then_inc(lora_mm, 1)

            unit_steps(pe, unit_step)
            m = NG * NU - 1
            attend_scores(m)
            attend_ascores(m, NG)
            pe.wait_ge(turned[Q_], NG * NU)
            pe.wait_ge(turned[K_], NG * NU)
            pe.wait_ge(wp_lo_pool, PL)
            pe.wait_ge(wp_lo_dve, KC - PL)
            project_out(0, 0, KC)
            attend_transposes(m)
            attend_values(m, NG)
            project_out(1, 0, 6)
            pe.wait_ge(fconsts, 16 * NFCONST)
            pe.wait_ge(y_copied, NG * NU)
            pe.wait_ge(ashifted, NG * NU)
            pe.wait_ge(edges, 2)
            convolve(0)
            project_out(1, 6, KC)

            def pair_step(p, ahead):
                if ahead >= 2:
                    for c in range(KC):
                        last_layer(p, (2, 0, 1), c)
                    project_out(p + 2, 0, 3)
                    turn_hidden(p)
                    project_out(p + 2, 3, 5)
                    low_rank(p)
                    convolve(p + 1)
                    project_out(p + 2, 5, KC)
                    return
                for k in (2, 0, 1):
                    if k == 1:
                        turn_hidden(p)
                    for c in range(KC):
                        last_layer(p, (k,), c)
                if ahead == 1:
                    convolve(p + 1)
                low_rank(p)

            pair_steps(pe, pair_step)

        @block.scalar
        def _(act):
            mix_scalar(act)
            act.wait_ge(consts, 16 * NCONST)
            act.wait_ge(cleared, NCLEAR)
            act.activation(wte2_parts[:, :, 0, :], wte[:], ACT.Copy).then_inc(wte_hi, 1)

            def split_hi(x, g, n):
                act.wait_ge(w_in, 16 * g + 16)
                wait(act, mm_done[x], n)
                if x != Q_:
                    wait(act, akv_mm, g)
                act.activation(whi[:, :, x, :], wst[:, :, x, :], ACT.Copy).then_inc(w_hi[x], 1)

            def attend_exp(m):
                for t in range(2):
                    act.wait_ge(shifted, 2 * m + t + 1)
                    act.activation(prob[t][:], prob[t][:], ACT.Exp, scale=SCALE).then_inc(exped, 1)
                act.wait_ge(ashifted, m + 1)
                act.activation(atmp[:], atmp[:], ACT.Exp, scale=ASCALE).then_inc(aexped, 1)

            def attend_copies(m):
                act.wait_ge(a_tr, m + 1)
                wait(act, y_mm, m)
                act.activation(aT[:], bS[0][:], ACT.Copy).then_inc(aT_copied, 1)
                for t, src in ((0, bPT), (1, bS[1])):
                    act.wait_ge(p_tr, 2 * m + t + 1)
                    act.activation(pT[t][:].rearrange("p s h q -> p (s h q)"), src[:], ACT.Copy).then_inc(pT_copied, 1)

            def y_copy(m):
                act.wait_ge(y_mm, m + 1)
                wait(act, y_out, 16 * m)
                act.activation(ysb[:], bY[:], ACT.Copy).then_inc(y_copied, 1)

            def wproj_hi(c0, c1):
                for c in range(c0, c1):
                    act.wait_ge(mm_done[V_], NU * (NG - 1) + 2)
                    act.wait_ge(wp_in, 16 * KC)
                    act.activation(wphi[:, c, :], wp_raw[:, c, :], ACT.Copy).then_inc(wp_hi, 1)

            def wffn_hi(i0, i1):
                for i in range(i0, i1):
                    act.wait_ge(mm_done[V_], NU * NG)
                    act.wait_ge(wf_in[i % NST], 16 * (i // NST + 1))
                    act.activation(wfhi[:, i, :], wf_raw[i % NST], ACT.Copy).then_inc(wf_hi_set, 1)

            def split_y(p):
                act.wait_ge(y_in, 16 * (p + 1))
                wait(act, proj_mm, p)
                act.activation(yhi[:], yst[:], ACT.Copy).then_inc(y_hi, 1)

            def split_conv(p):
                wait(act, ffn_mm, p)
                for b in range(2):
                    act.wait_ge(conv_set, 2 * p + b + 1)
                    act.activation(chi[:, :, NC * b:NC * (b + 1)], ct[:, :, NC * b:NC * (b + 1)], ACT.Copy
                                   ).then_inc(c_hi, 1)

            def route_and_copy(p):
                act.wait_ge(route, ROUTE_EXP + ROUTE_ALL * p)
                act.activation(rs[:, 1:2], rs[:, 0:1], ACT.Exp).then_inc(route_exp, 1)
                act.wait_ge(hw_tr, p + 1)
                wait(act, lora_mm, 2 * p)
                act.activation(hwThi[:], bT[:, 0:P], ACT.Copy).then_inc(hwT_hi, 1)

            def unit_step(g, u):
                n = NU * g + u
                att = not first(g, u)
                if att:
                    attend_exp(n - 1)
                act.wait_ge(rotated[K_], n + 1)
                wait(act, scores, 2 * n)
                for h in range(GH):
                    cp = act.activation(kbd[HD * h:HD * (h + 1), :, h, :],
                                        kr[HD * h:HD * (h + 1), :].rearrange("p (b k) -> p b k", k=NC), ACT.Copy)
                cp.then_inc(kbd_set, 1)
                if refill(g, u):
                    split_hi(K_, g + 1, n + 1)
                if att:
                    attend_copies(n - 1)
                if last(g) and u == 2:
                    wproj_hi(0, 4)
                if last(g) and u == NU - 1:
                    split_y(0)
                if refill(g, u):
                    split_hi(Q_, g + 1, n + 1)
                act.wait_ge(mm_done[V_], n + 1)
                wait(act, v_tr, n)
                act.activation(vT[:], bV[:], ACT.Copy).then_inc(vT_copied, 1)
                if refill(g, u):
                    split_hi(V_, g + 1, n + 1)
                if u == 0:
                    act.wait_ge(akv_mm, g + 1)
                    wait(act, ak_tr, g)
                    act.activation(akv[:], bAD[0:2 * NA, 0:2 * P], ACT.Copy).then_inc(akv_copied, 1)
                if att:
                    y_copy(n - 1)
                if u == 0:
                    act.wait_ge(avs_set, g + 1)
                    wait(act, ascores, n)
                    for h in range(GH):
                        cp = act.activation(akbd[HD * h:HD * (h + 1), h, :], bAD[HD * h:HD * (h + 1), AKT:AKT + NA],
                                            ACT.Copy)
                    cp.then_inc(akbd_set, 1)
                act.wait_ge(v_tr, n + 1)
                wait(act, y_mm, n)
                for b in range(2):
                    for h in range(2):
                        cp = act.activation(
                            vbd[NC * h:NC * (h + 1), :, b, :, HD * h:HD * (h + 1)],
                            bV[NC * b:NC * (b + 1), :].rearrange("p (s a h e) -> p s a h e", s=UP, a=2, h=2)[:, :, :, h, :],
                            ACT.Copy)
                cp.then_inc(vbd_set, 1)
                if last(g) and u == 2:
                    wproj_hi(4, KC)

            unit_steps(act, unit_step)
            wffn_hi(0, 1)
            m = NG * NU - 1
            attend_exp(m)
            wffn_hi(1, 4)
            attend_copies(m)
            split_y(1)
            y_copy(m)
            wffn_hi(4, KC - 1)
            act.wait_ge(y_out, 16 * NG * NU)
            act.wait_ge(fconsts, 16 * NFCONST)
            act.activation(loraBhi[:], loraB[:], ACT.Copy).then_inc(lora_hi, 1)
            wffn_hi(KC - 1, KC)
            split_conv(0)

            def pair_step(p, ahead):
                if ahead >= 2:
                    split_y(p + 2)
                route_and_copy(p)
                if ahead >= 1:
                    split_conv(p + 1)

            pair_steps(act, pair_step)

        @block.vector
        def _(dve):
            mix_vector(dve)
            wait_z(dve, NU)
            dve.memset(x8[0:P // 2, :, 0:1], 0.0).then_inc(edges, 1)
            dve.memset(x8[P // 2:P, :, L // PH:L // PH + 1], 0.0).then_inc(edges, 1)
            dve.wait_ge(wte_hi, 1)
            dve.tensor_tensor(wte2_parts[:, :, 1, :], wte[:], wte2_parts[:, :, 0, :].bitcast(F32), ALU.subtract
                              ).then_inc(wte_lo, 1)

            def split_lo(x, g, n):
                dve.wait_ge(w_hi[x], g + 1)
                wait(dve, mm_done[x], n)
                if x != Q_:
                    wait(dve, akv_mm, g)
                dve.tensor_tensor(wlo[:, :, x, :], wst[:, :, x, :], whi_f[:, :, x, :], ALU.subtract
                                  ).then_inc(w_lo[x], 1)

            def rotate(x, src, dst, n, used, count):
                tab = [t[:].rearrange("p (a k) -> p a k", a=1).broadcast_to([P, UB, NC]) for t in (cosT, sinT)]
                i = 0 if x == K_ else 2
                dve.wait_ge(mm_done[x], n + 1)
                wait(dve, rotated[Q_ if x == K_ else K_], n if x == K_ else n + 1)
                for s, c in used:
                    wait(dve, s, c)
                dve.tensor_tensor(dst[:].rearrange("p (b k) -> p b k", k=NC),
                                  src[:].rearrange("p (b k) -> p b k", k=NC), tab[0], ALU.mult).then_inc(rot_step, 1)
                dve.stream_shuffle(rot[:], src[:], HALF_SWAP).then_inc(turned[x], 1)
                dve.wait_ge(turned[x], n + 1)
                r = rot[:].rearrange("p (b k) -> p b k", k=NC)
                dve.tensor_tensor(r, r, tab[1], ALU.mult).then_inc(rot_step, 1)
                dve.wait_ge(rot_step, 4 * n + i + 2)
                dve.tensor_tensor(dst[:], dst[:], rot[:], ALU.add).then_inc(rotated[x], 1)

            def attend_softmax(m):
                maskb = mask[:].rearrange("p (a k) -> p a k", a=1).broadcast_to([P, 8, NC])

                def spread(t, k):
                    return stat[:, t, k, :].rearrange("p (a b) -> p a b", b=1).broadcast_to([P, 8, NC])

                def aspread(k):
                    return astat[:, k, :].rearrange("p (a b) -> p a b", b=1).broadcast_to([P, UP * GH, NA])

                for t in range(2):
                    dve.wait_ge(scores, 2 * m + t + 1)
                    wait(dve, p_tr, 2 * m)
                    dve.tensor_tensor(prob[t][:], bS[t][:].rearrange("p (a k) -> p a k", k=NC), maskb, ALU.add
                                      ).then_inc(masked, 1)
                    dve.wait_ge(masked, 2 * m + t + 1)
                    dve.tensor_reduce(stat[:, t, 0, :], prob[t][:], AX, ALU.max).then_inc(row_max, 1)
                    dve.wait_ge(row_max, 2 * m + t + 1)
                    dve.tensor_tensor(prob[t][:], prob[t][:], spread(t, 0), ALU.subtract).then_inc(shifted, 1)
                dve.wait_ge(ascores, m + 1)
                asrc = bAD[:, 0:UP * GH * NA].rearrange("p (a k) -> p a k", k=NA)
                dve.tensor_reduce(astat[:, 0, :], asrc, AX, ALU.max).then_inc(amax, 1)
                dve.wait_ge(amax, m + 1)
                wait(dve, aprobs, m)
                dve.tensor_tensor(atmp[:], asrc, aspread(0), ALU.subtract).then_inc(ashifted, 1)
                for t in range(2):
                    dve.wait_ge(exped, 2 * m + t + 1)
                    dve.tensor_reduce(stat[:, t, 1, :], prob[t][:], AX, ALU.add).then_inc(row_sum, 1)
                    dve.wait_ge(row_sum, 2 * m + t + 1)
                    dve.reciprocal(stat[:, t, 2, :], stat[:, t, 1, :]).then_inc(inverted, 1)
                    dve.wait_ge(inverted, 2 * m + t + 1)
                    dve.tensor_tensor(prob[t][:], prob[t][:], spread(t, 2), ALU.mult).then_inc(probs, 1)
                dve.wait_ge(aexped, m + 1)
                dve.tensor_reduce(astat[:, 1, :], atmp[:], AX, ALU.add).then_inc(asum, 1)
                dve.wait_ge(asum, m + 1)
                dve.reciprocal(astat[:, 2, :], astat[:, 1, :]).then_inc(ainv, 1)
                dve.wait_ge(ainv, m + 1)
                dve.tensor_scalar(astat[:, 2, :], astat[:, 2, :], gate[:, 0:1], None, ALU.mult).then_inc(agated, 1)
                dve.wait_ge(agated, m + 1)
                wait(dve, a_tr, m)
                dve.tensor_tensor(atmp[:], atmp[:], aspread(2), ALU.mult).then_inc(aweighted, 1)
                dve.wait_ge(aweighted, m + 1)
                parts = aprob[:, :, 0:3 * AR].rearrange("p i (c k) -> p i c k", c=3)
                flat = atmp[:].rearrange("p (i h) a -> p i (h a)", i=UP)
                dve.tensor_copy(parts[:, :, 0:3:2, :],
                                flat.rearrange("p i (c k) -> p i c k", c=1).broadcast_to([P, UP, 2, AR])
                                ).then_inc(aprob_hi, 1)
                dve.wait_ge(aprob_hi, m + 1)
                dve.tensor_tensor(aprob[:, :, AR:2 * AR], flat, aprob[:, :, 0:AR].bitcast(F32), ALU.subtract
                                  ).then_inc(aprobs, 1)

            def wproj_lo(c0, c1):
                for c in range(c0, c1):
                    dve.wait_ge(mm_done[V_], NU * NG - 1)
                    dve.wait_ge(wp_hi, c + 1)
                    dve.tensor_tensor(wplo[:, c, :], wp_raw[:, c, :], wphi[:, c, :].bitcast(F32), ALU.subtract
                                      ).then_inc(wp_lo_dve, 1)

            def wffn_lo(i):
                dve.wait_ge(wf_hi_set, i + 1)
                dve.tensor_tensor(wflo[:, i, :], wf_raw[i % NST], wfhi[:, i, :].bitcast(F32), ALU.subtract
                                  ).then_inc(wf_lo_dve, 1)

            def split_y(p):
                dve.wait_ge(y_hi, p + 1)
                wait(dve, proj_mm, p)
                dve.tensor_tensor(ylo[:], yst[:], yhi[:].bitcast(F32), ALU.subtract).then_inc(y_lo, 1)

            def residual(p):
                dve.wait_ge(proj_mm, p + 1)
                dve.wait_ge(x_in, 16 * (p + 1))
                wait(dve, x1b_set, p)
                wait(dve, x1_out, 16 * p)
                dve.tensor_tensor(x1[:].rearrange("p (q m) -> p m q", q=PH), bP.rearrange("p (m q) -> p m q", q=PH),
                                  xt[:].rearrange("p (m q) -> p m q", q=PH), ALU.add).then_inc(x1_set, 1)

            def convolved(p):
                wait(dve, c_lo, 2 * p)
                wait(dve, ffn_mm, p)
                for b in range(2):
                    tokens = slice(NC * b, NC * (b + 1))
                    dve.wait_ge(conv_mm, 2 * p + b + 1)
                    dve.tensor_tensor(
                        ct[:, :, tokens].rearrange("p q (g o) -> p g q o", g=CONV),
                        bC[:, 512 * b:512 * (b + 1)].rearrange("p (g q o) -> p g q o", g=CONV, q=PH),
                        ctxb[:, ds(p * P + b * NC, NC)].rearrange("p (g a o) -> p g a o", g=CONV, a=1)
                        .broadcast_to([P, CONV, PH, CG]), ALU.add).then_inc(conv_set, 1)
                    dve.wait_ge(c_hi, 2 * p + b + 1)
                    dve.tensor_tensor(clo[:, :, tokens], ct[:, :, tokens], chi[:, :, tokens].bitcast(F32), ALU.subtract
                                      ).then_inc(c_lo, 1)

            def router(p):
                base = ROUTE_ALL * p
                count = [0]

                def then(ins):
                    ins.then_inc(route, 1)
                    count[0] += 1
                    dve.wait_ge(route, base + count[0])

                dve.wait_ge(hidden_mm, p + 1)
                dve.tensor_copy(lg[:], bF[:, HID + P:HID + P + NE]).then_inc(route, 1)
                count[0] += 1
                then(dve.max(top[:], bF[:, HID + P:HID + P + NE]))
                dve.tensor_tensor(rs[:, 0:1], top[:, 1:2], top[:, 0:1], ALU.subtract).then_inc(route, 1)
                count[0] += 1
                assert count[0] == ROUTE_EXP
                then(dve.max_index(topi[:], top[:], lg[:]))
                then(dve.tensor_copy(rs[:, 4:6], topi[:, 0:2]))
                dve.wait_ge(route_exp, p + 1)
                then(dve.tensor_scalar(rs[:, 2:3], rs[:, 1:2], 1.0, None, ALU.add))
                then(dve.reciprocal(rs[:, 3:4], rs[:, 2:3]))
                then(dve.tensor_scalar(rs[:, 6:7], rs[:, 3:4], LORA_SCALE, None, ALU.mult))
                then(dve.tensor_tensor(rs[:, 7:8], rs[:, 1:2], rs[:, 6:7], ALU.mult))
                for k in range(2):
                    then(dve.tensor_scalar(we[:, k, :], iota[:], rs[:, 4 + k:5 + k], rs[:, 6 + k:7 + k],
                                           ALU.is_equal, ALU.mult))
                then(dve.tensor_tensor(we[:, 2, :], we[:, 0, :], we[:, 1, :], ALU.add))
                assert count[0] == ROUTE_ALL
                wait(dve, hw_tr, p)
                dve.tensor_tensor(hw[:].rearrange("p (e r) -> p e r", r=RANK),
                                  bF[:, HID:HID + P].rearrange("p (e r) -> p e r", r=RANK),
                                  we[:, 2, :].rearrange("p (e a) -> p e a", a=1).broadcast_to([P, NE, RANK]),
                                  ALU.mult).then_inc(hw_set, 1)
                dve.wait_ge(hwT_hi, p + 1)
                wait(dve, lora_mm, 2 * p)
                dve.tensor_tensor(hwTlo[:], bT[:, 0:P], hwThi[:].bitcast(F32), ALU.subtract).then_inc(hwT_set, 1)

            def finish(p):
                dve.wait_ge(lora_mm, 2 * p + 1)
                dve.wait_ge(x1b_set, p + 1)
                wait(dve, stored, 16 * p)
                dve.tensor_tensor(osb[:, 2 * CW:L], bF[:, 1024:HID], x1b[:, 2 * CW:L], ALU.add).then_inc(hidden_free, 1)
                dve.wait_ge(lora_mm, 2 * p + 2)
                dve.tensor_tensor(osb[:, 0:2 * CW].rearrange("p (a c) -> p a c", a=2),
                                  bF[:, 0:1024].rearrange("p (a c) -> p a c", a=2)[:, :, 0:CW],
                                  x1b[:, 0:2 * CW].rearrange("p (a c) -> p a c", a=2), ALU.add).then_inc(out_set, 1)

            def unit_step(g, u):
                n = NU * g + u
                if not first(g, u):
                    attend_softmax(n - 1)
                rotate(K_, bK, kr, n, ((kbd_set, n),), n)
                if refill(g, u):
                    split_lo(K_, g + 1, n + 1)
                if last(g) and u == NU - 1:
                    wproj_lo(PL, KC - 1)
                rotate(Q_, bQ, qr, n, ((scores, 2 * n), (ascores, n)), n)
                if refill(g, u):
                    split_lo(Q_, g + 1, n + 1)
                    split_lo(V_, g + 1, n + 1)
                if u == 0:
                    dve.wait_ge(ak_tr, g + 1)
                    wait(dve, avbd_set, g)
                    dve.tensor_tensor(avs[:], bAD[:, AVS:AVS + P], amask[:], ALU.mult).then_inc(avs_set, 1)
                    dve.wait_ge(avs_set, g + 1)
                    dve.tensor_scalar(avh[:], avs[:], alow[:, 0:1], None, ALU.mult).then_inc(avh_set, 1)
                    dve.wait_ge(avh_set, g + 1)
                    wait(dve, y_mm, n)
                    dve.tensor_tensor(avbd[:], avs[:], avh[:].bitcast(F32), ALU.subtract).then_inc(avbd_set, 1)
                if last(g) and u == NU - 1:
                    wproj_lo(KC - 1, KC)
                    split_y(0)

            unit_steps(dve, unit_step)
            attend_softmax(NG * NU - 1)
            wffn_lo(WF_DVE[0])
            residual(0)
            split_y(1)
            wffn_lo(WF_DVE[1])
            dve.wait_ge(fconsts, 16 * NFCONST)
            dve.wait_ge(ctxb_in, 16)
            dve.wait_ge(wp_lo_dve, KC - PL)
            convolved(0)
            wffn_lo(WF_DVE[2])
            residual(1)
            dve.wait_ge(y_out, 16 * NG * NU)
            dve.wait_ge(lora_hi, 1)
            dve.tensor_tensor(loraBlo[:], loraB[:], loraBhi[:].bitcast(F32), ALU.subtract).then_inc(lora_lo, 1)

            def pair_step(p, ahead):
                if ahead >= 2:
                    split_y(p + 2)
                router(p)
                if ahead >= 2:
                    finish(p)
                if ahead >= 1:
                    convolved(p + 1)
                if ahead < 2:
                    finish(p)
                if ahead >= 2:
                    residual(p + 2)

            pair_steps(dve, pair_step)


ROUTE_EXP, ROUTE_ALL = 3, 12


def build(nc, d, out):
    y_dram = nc.dram_tensor("y_scratch", (NP, P, NG, P), F32).ap()
    ctx_dram = nc.dram_tensor("ctx_scratch", (1, TOK), F32).ap()
    x1_dram = nc.dram_tensor("x1_scratch", (NP, P, L), F32).ap()
    with ExitStack() as ctx:
        psum = ctx.enter_context(nc.psum_tensor("psum", [P, 8 * 512], F32))
        zbase = -(-nc.sbuf_base // 32) * 32
        z = ctx.enter_context(nc.sbuf_tensor("z", [P, NU, 2, KC, UT], F32R))
        wst = ctx.enter_context(nc.sbuf_tensor("w_st", [P, KC, 3, P], F32))
        whi = ctx.enter_context(nc.sbuf_tensor("w_hi", [P, KC, 3, P], F32R))
        wlo = ctx.enter_context(nc.sbuf_tensor("w_lo", [P, KC, 3, P], F32R))
        w_in = ctx.enter_context(nc.semaphore("w_in"))
        w_his = {x: ctx.enter_context(nc.semaphore(f"w_hi_set{x}")) for x in (Q_, K_, V_)}
        w_los = {x: ctx.enter_context(nc.semaphore(f"w_lo_set{x}")) for x in (Q_, K_, V_)}
        weights = (wst, whi, wlo, whi[:, :, :, :].bitcast(F32), w_in, w_his, w_los)
        program(nc, d, psum, z, zbase, y_dram, x1_dram, ctx_dram, weights, out)


def constants():
    theta = (1.0 / 10000.0 ** (np.arange(0, HD, 2, dtype=np.float32) / HD)).astype(np.float32)
    angle = np.outer(np.arange(NC, dtype=np.float32), theta).astype(np.float32)
    cos = np.cos(angle).astype(np.float32).T
    sin = np.sin(angle).astype(np.float32).T
    q, k = np.arange(P)[:, None] % NC, np.arange(NC)[None, :]
    row, part = np.arange(P) % (GH * NA), np.arange(P) // (GH * NA)
    return {
        "asel": ((row[None, :] % NA == np.arange(2 * NA)[:, None] % NA) & (part < 3)[None, :]).astype(np.float32),
        "afold": np.tile(np.eye(NA, dtype=np.float32), (2, 1)),
        "alow": (part == 2)[:, None].astype(np.float32),
        "amask": ((row[:, None] // NA == np.arange(P)[None, :] // HD) & (part < 3)[:, None]).astype(np.float32),
        "cos": np.tile(np.concatenate([cos, cos], 0), (GH, 1)),
        "sin": np.tile(np.concatenate([-sin, sin], 0), (GH, 1)),
        "mask": np.where(k <= q, 0.0, -1e30).astype(np.float32),
        "ident": np.eye(P, dtype=np.float32),
        "iota": np.tile(np.arange(NE, dtype=np.float32), (P, 1)),
    }


def layouts(v):
    w = v["L0_cond2_weight"]
    toep = np.zeros((P, CONV, 2, P), np.float32)
    for g in range(CONV):
        for j in range(2):
            for f in range(PH):
                for q in range(PH):
                    tap = PH * j + f - q
                    if 0 <= tap < TAPS:
                        toep[f * CG:(f + 1) * CG, g, j, q * CG:(q + 1) * CG] = w[g * CG:(g + 1) * CG, :, tap].T
    last = np.concatenate([v["L0_ffn_W_base"], v["L0_ffn_A"].reshape(NE * RANK, L), v["L0_ffn_W_router"]], 0)
    return {
        "x": v["x"],
        "mlp": np.concatenate([v["cond_128"].T, v["L0_cond_W0"], v["L0_cond_b0"][:, None], v["L0_cond_W1"],
                               v["L0_cond_b1"][:, None], v["L0_cond_W2"], v["L0_cond2_c_weight"].T], 1),
        "b2": v["L0_cond_b2"][None],
        "mix": np.concatenate([
            v["L0_cond_weight"][..., 0].reshape(NM, OB, P // NM, NC).transpose(2, 0, 1, 3).reshape(P, OB * NC),
            v["L0_cond_bias_k"].reshape(NM, OB, P // NM).transpose(2, 0, 1).reshape(P, OB),
            np.repeat(np.eye(P // NM, dtype=np.float32), NM, 0)], 1),
        "wqkvT": v["L0_attn_w_attn"].reshape(3, NG, P, KC, P).transpose(1, 4, 3, 0, 2),
        "wteT": v["L0_attn_adapter_wte"].reshape(NA, KC, P).transpose(2, 1, 0),
        "gate": np.broadcast_to(v["L0_attn_gating"], (P, 1)),
        "wprojT": v["L0_attn_w_proj"].T.reshape(KC, P, L),
        "wffnT": last.T.reshape(P, PH, NF).transpose(1, 0, 2),
        "loraB": v["L0_ffn_B"].transpose(0, 2, 1).reshape(NE * RANK, L),
        "toep": toep,
        "bbase": np.broadcast_to(v["L0_ffn_b_base"], (P, L)),
        "fside": np.broadcast_to(v["fside_S_0"], (NB, NC)),
    }


def kernel(**inputs):
    import concourse.bacc as bacc
    from concourse.bass_utils import run_bass_kernel_spmd as run

    nc = bacc.Bacc("TRN2", target_bir_lowering=False, num_devices=1, dynamic_dma_scratch_size=DMA_RING)
    arrays, d = {}, {}
    for name, a in {**layouts({k: np.asarray(a) for k, a in inputs.items()}), **constants()}.items():
        a = np.ascontiguousarray(a)
        arrays[f"in_{name}"] = a
        d[name] = nc.dram_tensor(f"in_{name}", a.shape, mybir.dt.from_np(a.dtype), kind="ExternalInput").ap()
    out = nc.dram_tensor("out_0", (NB, NC, L), F32, kind="ExternalOutput").ap()
    build(nc, d, out)
    r = run(nc, [arrays], core_ids=[0])
    return r.results[0]["out_0"]
```
